# Optimizing a Trainium2 kernel written in Bass

```python
import numpy as np
import jax
import jax.numpy as jnp

def _softmax(x, axis=-1):
    return jax.nn.softmax(x, axis=axis)

def _gelu(x):
    return jax.nn.gelu(x, approximate=True)

def _silu(x):
    return jax.nn.silu(x)

def _sigmoid(x):
    return jax.nn.sigmoid(x)

def _layernorm(x, axis=-1, eps=1e-05):
    m = jnp.mean(x, axis=axis, keepdims=True)
    v = jnp.var(x, axis=axis, keepdims=True)
    return (x - m) / jnp.sqrt(v + eps)

def _scatter_add(tgt, idx, src, axis=0):
    return tgt.at[idx].add(src)

def _segment_sum(src, seg, n):
    return jax.ops.segment_sum(src, seg, n)
kernel_name = 'mk_decoder_postln_d1_seqx_r8_56c187'

def setup_inputs(seed: int=0):
    np.random.seed(seed)
    _w = jnp.asarray

    def _rec_inputs():
        import jax
        import jax.numpy as jnp
        _rk = jax.random.key(seed)
        x = -0.0003929 + 0.9999 * jax.random.normal(jax.random.fold_in(_rk, 1), (16, 128, 128), jnp.float32)
        _lenS = 128 - jax.random.randint(jax.random.fold_in(_rk, 7), (16,), 0, max(1, 128 // 4) + 1, jnp.int32)
        _lenS2 = 128 - jax.random.randint(jax.random.fold_in(_rk, 8), (16,), 0, max(1, 128 // 4) + 1, jnp.int32)
        _ctx_1024P = jax.random.normal(jax.random.fold_in(_rk, 11), (16, 16, 128), jnp.float32)
        _ctx_1024c = jax.random.dirichlet(jax.random.fold_in(_rk, 511), 0.3 * jnp.ones((16,), jnp.float32), (16, 128))
        _ctx_1024t = jnp.einsum('bsk,bkd->bsd', _ctx_1024c, _ctx_1024P)
        _ctx_1024t = _ctx_1024t * jax.lax.rsqrt(jnp.mean(jnp.square(_ctx_1024t)) + 1e-12) * 0.953939
        ctx_1024 = 2.81802e-05 + 1.00001 * (_ctx_1024t + 0.3 * jax.random.normal(jax.random.fold_in(_rk, 611), (16, 128, 128), jnp.float32))
        return (x, ctx_1024)
    x, ctx_1024 = _rec_inputs()

    def _L0_attn_setup():
        import jax, jax.numpy as jnp
        import numpy as np
        B, T, D = (4, 256, 128)
        H, Dh = (16, 64)
        key = jax.random.key(seed)
        ks = jax.random.split(key, 5)
        std_qkv = float(np.sqrt(2.0 / (Dh * D)))
        std_o = float(np.sqrt(2.0 / (D * Dh)))
        return {'x': jax.random.normal(ks[0], (B, T, D), dtype=jnp.float32), 'W_Q': jax.random.normal(ks[1], (H, Dh, D), dtype=jnp.float32) * std_qkv, 'b_Q': jnp.zeros((H, Dh), dtype=jnp.float32), 'W_K': jax.random.normal(ks[2], (H, Dh, D), dtype=jnp.float32) * std_qkv, 'b_K': jnp.zeros((H, Dh), dtype=jnp.float32), 'W_V': jax.random.normal(ks[3], (H, Dh, D), dtype=jnp.float32) * std_qkv, 'b_V': jnp.zeros((H, Dh), dtype=jnp.float32), 'W_O': jax.random.normal(ks[4], (H, D, Dh), dtype=jnp.float32) * std_o, 'b_O': jnp.zeros((D,), dtype=jnp.float32)}
    _L0_attn_all = _L0_attn_setup()
    _L0_attn_in = {k: v for k, v in _L0_attn_all.items() if k in ('W_Q', 'b_Q', 'W_K', 'b_K', 'W_V', 'b_V', 'W_O', 'b_O')}
    del _L0_attn_all

    def _L0_xattn_setup():
        import math
        import jax, jax.numpy as jnp
        import numpy as np
        D_MODEL, N_HEADS, D_K = (128, 16, 64)
        B, S = (4, 512)
        key = jax.random.key(seed)
        ks = jax.random.split(key, 11)
        scale = 1.0 / math.sqrt(D_MODEL)
        hd = N_HEADS * D_K
        return {'query': jax.random.normal(ks[0], (B, S, D_MODEL), jnp.float32), 'key': jax.random.normal(ks[1], (B, S, D_MODEL), jnp.float32), 'value': jax.random.normal(ks[2], (B, S, D_MODEL), jnp.float32), 'Wq': jax.random.normal(ks[3], (hd, D_MODEL), jnp.float32) * scale, 'bq': jnp.zeros((hd,), jnp.float32), 'Wk': jax.random.normal(ks[4], (hd, D_MODEL), jnp.float32) * scale, 'bk': jnp.zeros((hd,), jnp.float32), 'Wv': jax.random.normal(ks[5], (hd, D_MODEL), jnp.float32) * scale, 'bv': jnp.zeros((hd,), jnp.float32), 'Wo': jax.random.normal(ks[6], (D_MODEL, hd), jnp.float32) * scale, 'bo': jnp.zeros((D_MODEL,), jnp.float32)}
    _L0_xattn_all = _L0_xattn_setup()
    _L0_xattn_in = {k: v for k, v in _L0_xattn_all.items() if k in ('Wq', 'bq', 'Wk', 'bk', 'Wv', 'bv', 'Wo', 'bo')}
    del _L0_xattn_all

    def _L0_ffn_setup():
        import jax, jax.numpy as jnp
        import numpy as np
        DIM = 128
        NUM_HEAVY = 128
        N_ITERS = 50
        EPS = 1.0
        FETCH_K_RATIO = 9.0 / 8.0

        def rms_norm(x, gamma):
            norm = jnp.maximum(jnp.linalg.norm(x, axis=-1, keepdims=True), 1e-12)
            return x / norm * x.shape[-1] ** 0.5 * gamma

        def feed_forward(x, gamma, w1, b1, w2, b2):
            h = jax.nn.gelu(rms_norm(x, gamma) @ w1 + b1, approximate=False)
            return h @ w2 + b2

        def coor_descent(s, k, n_iters, eps):
            logk = jnp.log(jnp.asarray(k, dtype=s.dtype))

            def step(ab, _):
                a, b = ab
                sb = (s + b) / eps
                a = eps * (logk - jax.scipy.special.logsumexp(sb, axis=-1, keepdims=True))
                b = -jax.nn.relu(s + a)
                return ((a, b), None)
            a0 = jnp.zeros_like(s[..., :1])
            b0 = -s
            (a, b), _ = jax.lax.scan(step, (a0, b0), None, length=n_iters)
            return jnp.exp((s + a + b) / eps)
        key = jax.random.key(seed)
        ks = jax.random.split(key, 8)
        b, n, d = (4, 1024, DIM)
        dl, dh = (int(d * 0.5), d * 4)
        u = lambda k, shape, fan_in: jax.random.uniform(k, shape, jnp.float32, -1.0, 1.0) / np.sqrt(fan_in)
        return {'x': jax.random.normal(ks[0], (b, n, d), jnp.float32), 'routing_token': jax.random.normal(ks[1], (d,), jnp.float32), 'light_gamma': jnp.ones((d,), jnp.float32), 'light_w1': u(ks[2], (d, dl), d), 'light_b1': jnp.zeros((dl,), jnp.float32), 'light_w2': u(ks[3], (dl, d), dl), 'light_b2': jnp.zeros((d,), jnp.float32), 'heavy_gamma': jnp.ones((d,), jnp.float32), 'heavy_w1': u(ks[4], (d, dh), d), 'heavy_b1': jnp.zeros((dh,), jnp.float32), 'heavy_w2': u(ks[5], (dh, d), dh), 'heavy_b2': jnp.zeros((d,), jnp.float32)}
    _L0_ffn_all = _L0_ffn_setup()
    _L0_ffn_in = {k: v for k, v in _L0_ffn_all.items() if k in ('routing_token', 'light_gamma', 'light_w1', 'light_b1', 'light_w2', 'light_b2', 'heavy_gamma', 'heavy_w1', 'heavy_b1', 'heavy_w2', 'heavy_b2')}
    del _L0_ffn_all
    return {'x': x, 'ctx_1024': ctx_1024, 'L0_attn_W_Q': _L0_attn_in['W_Q'], 'L0_attn_b_Q': _L0_attn_in['b_Q'], 'L0_attn_W_K': _L0_attn_in['W_K'], 'L0_attn_b_K': _L0_attn_in['b_K'], 'L0_attn_W_V': _L0_attn_in['W_V'], 'L0_attn_b_V': _L0_attn_in['b_V'], 'L0_attn_W_O': _L0_attn_in['W_O'], 'L0_attn_b_O': _L0_attn_in['b_O'], 'L0_xattn_Wq': _L0_xattn_in['Wq'], 'L0_xattn_bq': _L0_xattn_in['bq'], 'L0_xattn_Wk': _L0_xattn_in['Wk'], 'L0_xattn_bk': _L0_xattn_in['bk'], 'L0_xattn_Wv': _L0_xattn_in['Wv'], 'L0_xattn_bv': _L0_xattn_in['bv'], 'L0_xattn_Wo': _L0_xattn_in['Wo'], 'L0_xattn_bo': _L0_xattn_in['bo'], 'L0_ffn_routing_token': _L0_ffn_in['routing_token'], 'L0_ffn_light_gamma': _L0_ffn_in['light_gamma'], 'L0_ffn_light_w1': _L0_ffn_in['light_w1'], 'L0_ffn_light_b1': _L0_ffn_in['light_b1'], 'L0_ffn_light_w2': _L0_ffn_in['light_w2'], 'L0_ffn_light_b2': _L0_ffn_in['light_b2'], 'L0_ffn_heavy_gamma': _L0_ffn_in['heavy_gamma'], 'L0_ffn_heavy_w1': _L0_ffn_in['heavy_w1'], 'L0_ffn_heavy_b1': _L0_ffn_in['heavy_b1'], 'L0_ffn_heavy_w2': _L0_ffn_in['heavy_w2'], 'L0_ffn_heavy_b2': _L0_ffn_in['heavy_b2']}

def reference(x, ctx_1024, L0_attn_W_Q, L0_attn_b_Q, L0_attn_W_K, L0_attn_b_K, L0_attn_W_V, L0_attn_b_V, L0_attn_W_O, L0_attn_b_O, L0_xattn_Wq, L0_xattn_bq, L0_xattn_Wk, L0_xattn_bk, L0_xattn_Wv, L0_xattn_bv, L0_xattn_Wo, L0_xattn_bo, L0_ffn_routing_token, L0_ffn_light_gamma, L0_ffn_light_w1, L0_ffn_light_b1, L0_ffn_light_w2, L0_ffn_light_b2, L0_ffn_heavy_gamma, L0_ffn_heavy_w1, L0_ffn_heavy_b1, L0_ffn_heavy_w2, L0_ffn_heavy_b2):
    import jax
    import jax.numpy as jnp

    def _L0_attn_ref(x, W_Q, b_Q, W_K, b_K, W_V, b_V, W_O, b_O):
        import jax, jax.numpy as jnp
        import numpy as np
        B, T, D = (4, 256, 128)
        H, Dh = (16, 64)
        Q = jnp.einsum('btd,hkd->bthk', x, W_Q) + b_Q
        K = jnp.einsum('btd,hkd->bthk', x, W_K) + b_K
        V = jnp.einsum('btd,hkd->bthk', x, W_V) + b_V
        d_head = W_Q.shape[1]
        scores = jnp.einsum('bqhk,bshk->bhqs', Q, K) / jnp.sqrt(jnp.asarray(d_head, x.dtype))
        attn = jax.nn.softmax(scores, axis=-1)
        out_h = jnp.einsum('bhqs,bshk->bqhk', attn, V)
        return jnp.einsum('bqhk,hdk->bqd', out_h, W_O) + b_O

    def _L0_xattn_ref(query, key, value, Wq, bq, Wk, bk, Wv, bv, Wo, bo):
        import math
        import jax, jax.numpy as jnp
        import numpy as np
        D_MODEL, N_HEADS, D_K = (128, 16, 64)
        B, S = (4, 512)
        b, s, _ = query.shape
        q = (query @ Wq.T + bq).reshape(b, s, N_HEADS, D_K)
        k = (key @ Wk.T + bk).reshape(b, s, N_HEADS, D_K)
        v = (value @ Wv.T + bv).reshape(b, s, N_HEADS, D_K)
        inv_sqrt_dk = 1.0 / math.sqrt(D_K)
        scores = jnp.einsum('bshd,bsgd->bshg', q, k) * inv_sqrt_dk
        attn = jax.nn.softmax(scores, axis=-1)
        out = jnp.einsum('bshg,bsgd->bshd', attn, v)
        out = jnp.transpose(out, (0, 2, 1, 3)).reshape(b, -1, N_HEADS * D_K)
        return out @ Wo.T + bo

    def _L0_ffn_ref(x, routing_token, light_gamma, light_w1, light_b1, light_w2, light_b2, heavy_gamma, heavy_w1, heavy_b1, heavy_w2, heavy_b2):
        import jax, jax.numpy as jnp
        import numpy as np
        DIM = 128
        NUM_HEAVY = 128
        N_ITERS = 50
        EPS = 1.0
        FETCH_K_RATIO = 9.0 / 8.0

        def rms_norm(x, gamma):
            norm = jnp.maximum(jnp.linalg.norm(x, axis=-1, keepdims=True), 1e-12)
            return x / norm * x.shape[-1] ** 0.5 * gamma

        def feed_forward(x, gamma, w1, b1, w2, b2):
            h = jax.nn.gelu(rms_norm(x, gamma) @ w1 + b1, approximate=False)
            return h @ w2 + b2

        def coor_descent(s, k, n_iters, eps):
            logk = jnp.log(jnp.asarray(k, dtype=s.dtype))

            def step(ab, _):
                a, b = ab
                sb = (s + b) / eps
                a = eps * (logk - jax.scipy.special.logsumexp(sb, axis=-1, keepdims=True))
                b = -jax.nn.relu(s + a)
                return ((a, b), None)
            a0 = jnp.zeros_like(s[..., :1])
            b0 = -s
            (a, b), _ = jax.lax.scan(step, (a0, b0), None, length=n_iters)
            return jnp.exp((s + a + b) / eps)
        b, n, d = x.shape
        light_out = feed_forward(x, light_gamma, light_w1, light_b1, light_w2, light_b2)
        s = jnp.einsum('bnd,d->bn', x, routing_token)
        effective_k = min(NUM_HEAVY * FETCH_K_RATIO, n)
        scores = coor_descent(s, effective_k, N_ITERS, EPS)
        sel_scores, sel_idx = jax.lax.top_k(scores, NUM_HEAVY)
        sel_scores = sel_scores + jax.lax.stop_gradient(1.0 - sel_scores)
        routed = jnp.take_along_axis(x, sel_idx[..., None], axis=1)
        routed_out = feed_forward(routed, heavy_gamma, heavy_w1, heavy_b1, heavy_w2, heavy_b2)
        routed_out = routed_out * sel_scores[..., None]
        batch_idx = jnp.arange(b)[:, None]
        heavy_out = jnp.zeros_like(x).at[batch_idx, sel_idx].set(routed_out)
        return light_out + heavy_out
    x = _layernorm(x + _L0_attn_ref(x, L0_attn_W_Q, L0_attn_b_Q, L0_attn_W_K, L0_attn_b_K, L0_attn_W_V, L0_attn_b_V, L0_attn_W_O, L0_attn_b_O), axis=-1)
    x = _layernorm(x + _L0_xattn_ref(x, ctx_1024, ctx_1024, L0_xattn_Wq, L0_xattn_bq, L0_xattn_Wk, L0_xattn_bk, L0_xattn_Wv, L0_xattn_bv, L0_xattn_Wo, L0_xattn_bo), axis=-1)
    x = _layernorm(x + _L0_ffn_ref(x, L0_ffn_routing_token, L0_ffn_light_gamma, L0_ffn_light_w1, L0_ffn_light_b1, L0_ffn_light_w2, L0_ffn_light_b2, L0_ffn_heavy_gamma, L0_ffn_heavy_w1, L0_ffn_heavy_b1, L0_ffn_heavy_w2, L0_ffn_heavy_b2), axis=-1)
    return x

_drawn_inputs = setup_inputs


def setup_inputs(seed=0):
    import zlib

    import numpy as np

    out = dict(_drawn_inputs(seed))
    spreads = {'L0_attn_b_Q': (0.0, 0.8),
     'L0_attn_b_K': (0.0, 0.8),
     'L0_attn_b_V': (0.0, 0.1),
     'L0_attn_b_O': (0.0, 0.1),
     'L0_xattn_bq': (0.0, 0.1),
     'L0_xattn_bk': (0.0, 0.1),
     'L0_xattn_bv': (0.0, 0.1),
     'L0_xattn_bo': (0.0, 0.1),
     'L0_ffn_light_gamma': (1.0, 0.2),
     'L0_ffn_light_b1': (0.0, 0.1),
     'L0_ffn_light_b2': (0.0, 0.1),
     'L0_ffn_heavy_gamma': (1.0, 0.2),
     'L0_ffn_heavy_b1': (0.0, 0.1),
     'L0_ffn_heavy_b2': (0.0, 0.1)}
    factors = {'L0_attn_W_Q': 8.0, 'L0_attn_W_K': 8.0, 'L0_attn_W_V': 8.0}
    for name, (base, spread) in spreads.items():
        noise = np.random.default_rng([zlib.crc32(name.encode()), seed]).standard_normal(out[name].shape)
        drawn = base * np.exp(spread * noise) if base else spread * noise
        out[name] = jnp.asarray(drawn.astype(out[name].dtype))
    for name, factor in factors.items():
        out[name] = (out[name] * factor).astype(out[name].dtype)
    return out
```

```python
from contextlib import ExitStack

import concourse.bass as bass
from concourse import mybir

B, T, D = 16, 128, 128
H, DH = 16, 64
HD = H * DH
NC = HD // 128
HALF = T // 2
IH, J, K = 2, 4, 8
FH, FL = 512, 64
NF = FH // 128 + 1
GB = 4
BANK = 512
EPS = 1e-5
RING = 18


def build(nc, x_nat, x_t, ctx_t, w_qk, w_v, w_o, b_qk, b_v, b_o,
          w2_q, w2_k, w2_v, w2_o, b2_q, b2_k, b2_v, b2_o,
          w_up, g_light, g_heavy, w_down, w_down_light, b_up, bd_light, bd_heavy,
          ident_in, perm_in, mask_in, out):
    fp32 = mybir.dt.float32
    ALU = mybir.AluOpType
    ACT = mybir.ActivationFunctionType
    AX = mybir.AxisListType

    ctx = ExitStack()
    with ctx:
        def sb(name, shape):
            return ctx.enter_context(nc.sbuf_tensor(name, shape, fp32))

        def sem(name):
            return ctx.enter_context(nc.semaphore(name))

        wqk = sb("wqk", [128, 2 * HD])
        wv = sb("wv", [128, HD])
        wo = sb("wo", [128, NC * D])
        wq2 = sb("wq2", [128, HD])
        wk2 = sb("wk2", [128, HD])
        wv2 = sb("wv2", [128, HD])
        wo2 = sb("wo2", [128, K * D])
        wup = sb("wup", [128, FH + FL])
        wdn = sb("wdn", [128, (NF - 1) * D])
        wdl = sb("wdl", [FL, D])
        bqk = sb("bqk", [128, 2 * NC])
        bv = sb("bv", [128, NC])
        bo_row = sb("bo_row", [128, D])
        bq2 = sb("bq2", [128, NC])
        bk2 = sb("bk2", [128, NC])
        bv2_row = sb("bv2_row", [128, HD])
        bo2_row = sb("bo2_row", [128, D])
        bup = sb("bup", [128, NF])
        bdl_row = sb("bdl_row", [128, D])
        bdh_row = sb("bdh_row", [128, D])
        gam = sb("gam", [128, 2])
        ident = sb("ident", [128, 128])
        perm = sb("perm", [128, 128])
        mask = sb("mask", [128, K])
        minus_half = sb("minus_half", [128, 4])
        eps = sb("eps", [128, 4])
        scratch = sb("scratch", [128, 1])

        xt = [sb(f"xt{i}", [128, T]) for i in range(2)]
        xres = [sb(f"xres{i}", [T, D]) for i in range(2)]
        ct = [sb(f"ct{i}", [128, T]) for i in range(2)]
        qt = sb("qt", [128, NC * T])
        kt = sb("kt", [128, NC * T])
        v = sb("v", [T, HD])
        p = sb("p", [T, H * T])
        neg_max = sb("neg_max", [T, H])
        row_sum = sb("row_sum", [T, H])
        row_inv = sb("row_inv", [T, H])
        pt = sb("pt", [T, H * T])
        ot = sb("ot", [128, NC * T])
        t1 = sb("t1", [T, D])
        st1 = sb("st1", [T, 6])
        mv1 = sb("mv1", [T, 2])
        ve1 = sb("ve1", [T, 1])
        rs1 = sb("rs1", [T, 1])
        x1 = sb("x1", [T, D])
        x1b = [sb(f"x1b{i}", [T, D]) for i in range(2)]
        x1t = sb("x1t", [128, T])
        qb = sb("qb", [128, HALF * 2 * H])
        kt2 = sb("kt2", [128, H * HALF])
        v2s = sb("v2s", [T, HD])
        v2 = sb("v2", [128, J * 2 * IH * DH])
        s2 = sb("s2", [128, IH * K * H])
        mx2 = sb("mx2", [128, IH * K])
        sum2 = sb("sum2", [128, IH * K])
        inv2 = sb("inv2", [128, IH * K])
        pb = sb("pb", [128, IH * J * 2 * K * H])
        ot2 = sb("ot2", [128, K * H * 8])
        t2 = sb("t2", [T, D])
        st2 = sb("st2", [T, 6])
        mv2 = sb("mv2", [T, 2])
        ve2 = sb("ve2", [T, 1])
        rs2 = sb("rs2", [T, 1])
        x2 = sb("x2", [T, D])
        sq = sb("sq", [T, D])
        ss = sb("ss", [T, 1])
        ssm = sb("ssm", [T, 1])
        rn = sb("rn", [T, 1])
        xn = sb("xn", [T, D])
        x2b = sb("x2b", [T, B * D])
        xnt = sb("xnt", [128, B * T])
        ht = [sb(f"ht{c}", [128, GB * T]) for c in range(NF)]
        t3 = sb("t3", [T, GB * D])
        st3 = sb("st3", [T, GB * 6])
        mv3 = sb("mv3", [T, GB * 2])
        ve3 = sb("ve3", [T, GB])
        rs3 = sb("rs3", [T, GB])

        ps = ctx.enter_context(nc.psum_tensor("ps", [128, 8 * BANK], fp32))

        def bank(n, cols=BANK, banks=1):
            return ps[:, n * BANK:n * BANK + (banks - 1) * BANK + cols]

        T_BANK = [7, 0, 1, 6]
        PV_BANK = [7, 0]
        V_BANK = [1, 6]
        S_BANK = [7, 0, 1, 6]
        X2T_BANK = 6
        QK, O, PT2, X1T, PV2, K2, Q2, O2, V2, S2 = 0, 4, 5, 6, 7, 9, 11, 13, 14, 16

        def ring(par, unit):
            return 2 + (RING * par + unit) % 4

        in_xt = [sem(f"in_xt{i}") for i in range(2)]
        in_xres = [sem(f"in_xres{i}") for i in range(2)]
        in_ct = [sem(f"in_ct{i}") for i in range(2)]
        in_wqk = [sem(f"in_wqk{i}") for i in range(4)]
        in_bqk = sem("in_bqk")
        in_wv = sem("in_wv")
        in_ident = sem("in_ident")
        in_bv = sem("in_bv")
        in_wo = sem("in_wo")
        in_bo = sem("in_bo")
        in_perm = sem("in_perm")
        in_wk2 = sem("in_wk2")
        in_wq2 = sem("in_wq2")
        in_bqk2 = sem("in_bqk2")
        in_wv2 = sem("in_wv2")
        in_bv2 = sem("in_bv2")
        in_mask = sem("in_mask")
        in_wo2 = sem("in_wo2")
        in_bo2 = sem("in_bo2")
        in_ffn = sem("in_ffn")
        v2_moved = sem("v2_moved")
        out_stored = sem("out_stored")
        mm_qk, mm_v, mm_s, mm_t, mm_pv, mm_o = (sem(n) for n in ("mm_qk", "mm_v", "mm_s", "mm_t", "mm_pv", "mm_o"))
        mm_x1t, mm_k2, mm_q2, mm_v2, mm_s2 = (sem(n) for n in ("mm_x1t", "mm_k2", "mm_q2", "mm_v2", "mm_s2"))
        mm_pt2, mm_pv2, mm_o2, mm_x2t = (sem(n) for n in ("mm_pt2", "mm_pv2", "mm_o2", "mm_x2t"))
        mm_h, mm_y = sem("mm_h"), sem("mm_y")
        qk_ready, v_ready, max_ready, exp_ready = (sem(n) for n in ("qk_ready", "v_ready", "max_ready", "exp_ready"))
        inv_ready, p_ready, pt_ready, ot_ready = (sem(n) for n in ("inv_ready", "p_ready", "pt_ready", "ot_ready"))
        xres_ready, sum1_ready, stats1_ready, mv1_ready = (sem(n) for n in ("xres_ready", "sum1_ready", "stats1_ready", "mv1_ready"))
        ve1_ready, rs1_ready, x1_ready, x1b_ready, x1t_ready = (sem(n) for n in ("ve1_ready", "rs1_ready", "x1_ready", "x1b_ready", "x1t_ready"))
        k2_ready, q2_ready, v2s_ready, s2_ready = (sem(n) for n in ("k2_ready", "q2_ready", "v2s_ready", "s2_ready"))
        mx2_ready, sub2_ready, exp2_ready, sum2_ready, inv2_ready, p2_ready = (
            sem(n) for n in ("mx2_ready", "sub2_ready", "exp2_ready", "sum2_ready", "inv2_ready", "p2_ready"))
        pb_ready, ot2_ready = sem("pb_ready"), sem("ot2_ready")
        sum2x_ready, stats2_ready, mv2_ready, ve2_ready, rs2_ready = (
            sem(n) for n in ("sum2x_ready", "stats2_ready", "mv2_ready", "ve2_ready", "rs2_ready"))
        x2_ready, ss_ready, ssm_ready, rn_ready, xn_ready, xnt_ready, x2b_ready = (
            sem(n) for n in ("x2_ready", "ss_ready", "ssm_ready", "rn_ready", "xn_ready", "xnt_ready", "x2b_ready"))
        zeroed, half_set, bq_scaled, wup_scaled, bd_summed = (sem(n) for n in ("zeroed", "half_set", "bq_scaled", "wup_scaled", "bd_summed"))
        ht_ready, y_banks_free, stats3_ready, mv3_ready, ve3_ready, rs3_ready, out_ready = (
            sem(n) for n in ("ht_ready", "y_banks_free", "stats3_ready", "mv3_ready", "ve3_ready", "rs3_ready", "out_ready"))

        block = ctx.enter_context(nc.Block())

        FIRST_LOOPED, LAST_LOOPED, LAST = 2, 13, B + 1

        def run_steps(eng, step):
            for s in range(FIRST_LOOPED):
                step(s, s // 2, s % 2, s < B, 1 <= s <= B, s >= 2, s < B - 1)
            with eng.Fori(0, (LAST_LOOPED + 1 - FIRST_LOOPED) // 2) as i:
                for par in range(2):
                    step(2 * i + (FIRST_LOOPED + par), i + FIRST_LOOPED // 2, par, True, True, True, True)
            for s in range(LAST_LOOPED + 1, LAST + 1):
                step(s, s // 2, s % 2, s < B, 1 <= s <= B, s >= 2, s < B - 1)

        @block.sync
        def _(sp):
            sp.dma_start(xt[0][:], x_t[0]).then_inc(in_xt[0], 16)
            for u in range(4):
                sp.dma_start(wqk[:, u * BANK:(u + 1) * BANK], w_qk[:, u * BANK:(u + 1) * BANK]).then_inc(in_wqk[u], 16)
            sp.dma_start(wv[:], w_v).then_inc(in_wv, 16)
            sp.dma_start(xt[1][:], x_t[1]).then_inc(in_xt[1], 16)
            sp.dma_start(wo[:], w_o).then_inc(in_wo, 16)
            sp.dma_start(wk2[:], w2_k).then_inc(in_wk2, 16)
            sp.dma_start(ct[0][:], ctx_t[0]).then_inc(in_ct[0], 16)
            sp.dma_start(wq2[:], w2_q).then_inc(in_wq2, 16)
            sp.dma_start(wv2[:], w2_v).then_inc(in_wv2, 16)
            sp.dma_start(wo2[:], w2_o).then_inc(in_wo2, 16)
            sp.dma_start(ct[1][:], ctx_t[1]).then_inc(in_ct[1], 16)

            def step(s, h, par, a, bc, d, load):
                b_par = 1 - par
                if load and bc:
                    sp.wait_ge(mm_v, 2 * s)
                    sp.dma_start(xt[b_par][:], x_t[bass.ds(s + 1, 1)].rearrange("b p t -> p (b t)")).then_inc(in_xt[b_par], 16)
                    sp.wait_ge(sum1_ready, s)
                    sp.dma_start(xres[b_par][:], x_nat[bass.ds(s + 1, 1)].rearrange("b p t -> p (b t)")).then_inc(in_xres[b_par], 16)
                if bc:
                    sp.wait_ge(v2s_ready, 2 * s)
                    for j in range(J):
                        for pp in range(2):
                            for ih in range(IH):
                                first = pp * HALF + ih * K * J + j
                                col = ((j * 2 + pp) * IH + ih) * DH
                                sp.dma_start(v2[:, col:col + DH],
                                             v2s[first:first + (K - 1) * J + 1:J, :].rearrange("k (g d) -> k g d", g=H)
                                             ).then_inc(v2_moved, 16)
                if load and bc:
                    sp.wait_ge(mm_v2, 2 * s)
                    sp.dma_start(ct[b_par][:], ctx_t[bass.ds(s + 1, 1)].rearrange("b p t -> p (b t)")).then_inc(in_ct[b_par], 16)

            run_steps(sp, step)
            with sp.Fori(0, B // GB) as g:
                sp.wait_ge(out_ready, g + 1)
                sp.dma_start(out[bass.ds(g * GB, GB)].rearrange("b t d -> t b d"),
                             x2b[:, bass.ds(g * (GB * D), GB * D)].rearrange("t (b d) -> t b d", b=GB)
                             ).then_inc(out_stored, 16)
            sp.wait_ge(out_stored, 16 * (B // GB))

        @block.gpsimd
        def _(pool):
            nc.gpsimd.memset(minus_half[:], -0.5).then_inc(half_set, 1)
            nc.gpsimd.memset(eps[:], EPS).then_inc(half_set, 1)
            nc.gpsimd.memset(qb[:], 0.0).then_inc(zeroed, 1)
            pool.dma_start(bo_row[:], b_o.partition_broadcast(128)).then_inc(in_bo, 16)
            pool.dma_start(bo2_row[:], b2_o.partition_broadcast(128)).then_inc(in_bo2, 16)
            pool.dma_start(bv2_row[:], b2_v.partition_broadcast(128)).then_inc(in_bv2, 16)
            for tile, src in ((bdl_row[:], bd_light.partition_broadcast(128)), (bdh_row[:], bd_heavy.partition_broadcast(128)),
                              (gam[:, 0:1], g_light), (gam[:, 1:2], g_heavy), (wup[:], w_up),
                              (wdn[:], w_down), (wdl[:], w_down_light), (bup[:], b_up)):
                pool.dma_start(tile, src).then_inc(in_ffn, 16)
            pool.wait_ge(in_bo, 16)
            pool.wait_ge(in_ffn, 8 * 16)
            nc.gpsimd.tensor_tensor(bdl_row[:], bdl_row[:], bdh_row[:], ALU.add).then_inc(bd_summed, 1)
            pool.wait_ge(bd_summed, 1)
            pool.wait_ge(half_set, 2)
            pool.wait_ge(in_bo2, 16)

            def step(s, h, par, a, bc, d, load):
                b_par = 1 - par
                s2v = s2[:].rearrange("p (i g) -> p i g", g=H)
                if a:
                    pool.wait_ge(in_xres[par], 16 * (h + 1))
                    nc.gpsimd.tensor_tensor(xres[par][:], xres[par][:], bo_row[:], ALU.add).then_inc(xres_ready, 1)
                if d:
                    pool.wait_ge(mx2_ready, s - 1)
                    nc.gpsimd.tensor_tensor(s2v, s2v, mx2[:].unsqueeze(2).to_broadcast([128, IH * K, H]),
                                            ALU.subtract).then_inc(sub2_ready, 1)
                    pool.wait_ge(inv2_ready, s - 1)
                    nc.gpsimd.tensor_tensor(s2v, s2v, inv2[:].unsqueeze(2).to_broadcast([128, IH * K, H]),
                                            ALU.mult).then_inc(p2_ready, 1)
                if bc:
                    pool.wait_ge(mv1_ready, s)
                    nc.gpsimd.tensor_tensor(ve1[:], mv1[:, 1:2], eps[:, 0:1], ALU.add).then_inc(ve1_ready, 1)
                    pool.wait_ge(ve1_ready, s)
                    nc.gpsimd.tensor_tensor(rs1[:], ve1[:], minus_half[:, 0:1], ALU.pow).then_inc(rs1_ready, 1)
                    pool.wait_ge(x1_ready, s)
                    nc.gpsimd.tensor_tensor(x1b[b_par][:], x1[:], bo2_row[:], ALU.add).then_inc(x1b_ready, 1)
                if a:
                    for half in range(2):
                        pool.wait_ge(inv_ready, 2 * s + half + 1)
                        ph = p[:, half * 8 * T:(half + 1) * 8 * T].rearrange("q (h k) -> q h k", h=8)
                        nc.gpsimd.tensor_tensor(ph, ph, row_inv[:, 8 * half:8 * half + 8].unsqueeze(2).to_broadcast([T, 8, T]),
                                                ALU.mult).then_inc(p_ready, 1)
                if d:
                    pool.wait_ge(mv2_ready, s - 1)
                    nc.gpsimd.tensor_tensor(ve2[:], mv2[:, 1:2], eps[:, 0:1], ALU.add).then_inc(ve2_ready, 1)
                    pool.wait_ge(ve2_ready, s - 1)
                    nc.gpsimd.tensor_tensor(rs2[:], ve2[:], minus_half[:, 0:1], ALU.pow).then_inc(rs2_ready, 1)
                    pool.wait_ge(ssm_ready, s - 1)
                    nc.gpsimd.tensor_tensor(rn[:], ssm[:], minus_half[:, 0:1], ALU.pow).then_inc(rn_ready, 1)
                    nc.gpsimd.tensor_tensor(x2b[:, bass.ds((s - 2) * D, D)], x2[:], bdl_row[:], ALU.add).then_inc(x2b_ready, 1)

            run_steps(pool, step)
            with pool.Fori(0, B // GB) as g:
                pool.wait_ge(mv3_ready, g + 1)
                nc.gpsimd.tensor_tensor(ve3[:], mv3[:].rearrange("p (b m) -> p b m", m=2)[:, :, 1], eps[:], ALU.add).then_inc(ve3_ready, 1)
                pool.wait_ge(ve3_ready, g + 1)
                nc.gpsimd.tensor_tensor(rs3[:], ve3[:], minus_half[:], ALU.pow).then_inc(rs3_ready, 1)

        @block.scalar
        def _(act):
            for tile, src, s_in in ((bqk[:], b_qk, in_bqk), (xres[0][:], x_nat[0], in_xres[0]), (ident[:], ident_in, in_ident), (bv[:], b_v, in_bv),
                                    (perm[:], perm_in, in_perm), (bk2[:], b2_k, in_bqk2), (bq2[:], b2_q, in_bqk2),
                                    (mask[:], mask_in, in_mask), (xres[1][:], x_nat[1], in_xres[1])):
                act.dma_start(tile, src).then_inc(s_in, 16)

            def step(s, h, par, a, bc, d, load):
                b_par = 1 - par

                def transposed(u):
                    act.wait_ge(mm_t, 4 * s - 4 + u + 1)
                    nc.scalar.activation(pt[:, u * BANK:(u + 1) * BANK], bank(T_BANK[u]), ACT.Copy).then_inc(pt_ready, 1)

                def exponentials(q):
                    act.wait_ge(max_ready, 4 * s + q + 1)
                    for pos in range(4):
                        hd = 8 * (q // 2) + 2 * pos + q % 2
                        last = nc.scalar.activation(p[:, hd * T:(hd + 1) * T], bank(S_BANK[q])[:, pos * T:(pos + 1) * T], ACT.Exp,
                                                    bias=neg_max[:, hd:hd + 1], accum_out=row_sum[:, hd:hd + 1])
                    last.then_inc(exp_ready, 1)

                def regrouped(ih):
                    act.wait_ge(mm_pv2, 2 * (s - 2) + ih + 1)
                    nc.scalar.activation(
                        ot2[:].rearrange("p (k h e) -> p k h e", k=K, h=H)[:, :, :, ih * J:(ih + 1) * J].rearrange("p k h j -> p j k h"),
                        bank(ring(par, PV2 + ih)).rearrange("p (j k h) -> p j k h", j=J, k=K), ACT.Copy).then_inc(ot2_ready, 1)

                if bc:
                    transposed(0)
                    transposed(1)
                if d:
                    act.wait_ge(sub2_ready, s - 1)
                    nc.scalar.activation(s2[:], s2[:], ACT.Exp, scale=DH ** -0.5).then_inc(exp2_ready, 1)
                if bc:
                    transposed(2)
                    transposed(3)
                if a:
                    for u in range(2):
                        act.wait_ge(mm_v, 2 * s + u + 1)
                        nc.scalar.activation(v[:, u * BANK:(u + 1) * BANK], bank(V_BANK[u]), ACT.Copy).then_inc(v_ready, 1)
                    exponentials(0)
                    exponentials(1)
                if bc:
                    act.wait_ge(mm_x1t, s)
                    nc.scalar.activation(x1t[:], bank(ring(par, X1T), T), ACT.Copy).then_inc(x1t_ready, 1)
                if a:
                    exponentials(2)
                if d:
                    regrouped(0)
                if a:
                    exponentials(3)
                if d:
                    regrouped(1)
                    act.wait_ge(rn_ready, s - 1)
                    nc.scalar.activation(xn[:], x2[:], ACT.Copy, scale=rn[:, 0:1]).then_inc(xn_ready, 1)
                if bc:
                    act.wait_ge(mm_s2, s)
                    sp2 = bank(ring(par, S2), BANK, 2).rearrange("p (i g j) -> p i g j", g=H, j=J)
                    for j in range(J):
                        last = nc.scalar.activation(s2[32 * j:32 * j + 32, :].rearrange("p (i g) -> p i g", g=H),
                                                    sp2[32 * j:32 * j + 32, :, :, j], ACT.Copy)
                    last.then_inc(s2_ready, 1)
                if d:
                    act.wait_ge(mm_x2t, s - 1)
                    nc.scalar.activation(xnt[:, bass.ds((s - 2) * T, T)], bank(X2T_BANK, T), ACT.Copy).then_inc(xnt_ready, 1)

            run_steps(act, step)
            act.wait_ge(in_ffn, 8 * 16)
            with act.Fori(0, B // GB) as g:
                for c in range(NF):
                    m = 128 if c < NF - 1 else FL
                    act.wait_ge(mm_h, NF * g + c + 1)
                    nc.scalar.activation(ht[c][0:m, :], bank(c % 4)[0:m, :], ACT.Gelu, bias=bup[0:m, c:c + 1]).then_inc(ht_ready, 1)

        @block.vector
        def _(dve):
            dve.wait_ge(in_bqk, 16)
            nc.vector.tensor_scalar(bqk[:, 0:NC], bqk[:, 0:NC], DH ** -0.5, None, ALU.mult).then_inc(bq_scaled, 1)
            dve.wait_ge(bq_scaled, 1)

            def step(s, h, par, a, bc, d, load):
                b_par = 1 - par

                def qk_out(u):
                    dst = (qt if u < 2 else kt)[:, (u % 2) * BANK:(u % 2 + 1) * BANK].rearrange("p (c t) -> p c t", c=4)
                    bias = bqk[:, 4 * u:4 * u + 4].unsqueeze(2).to_broadcast([128, 4, T])
                    src = bank(ring(par, QK + u)).rearrange("p (c t) -> p c t", c=4)
                    dve.wait_ge(mm_qk, 4 * s + u + 1)
                    nc.vector.scalar_tensor_tensor(out=dst, in0=src, scalar=DH ** -0.5 if u < 2 else 1.0, in1=bias,
                                                   op0=ALU.mult, op1=ALU.add).then_inc(qk_ready, 1)

                def halves_out(unit, u, bias_tile, dst):
                    src = bank(ring(par, unit + u)).rearrange("p (c e t) -> p c e t", c=4, e=2)
                    for h2 in range(2):
                        rows = slice(64 * h2, 64 * h2 + 64)
                        bias = bias_tile[rows, 4 * u:4 * u + 4]
                        for pp in range(2):
                            last = dst(u, h2, pp, src[rows, :, pp, :], bias)
                    return last

                def k2_dst(u, h2, pp, src, bias):
                    o = kt2[64 * pp:64 * pp + 64, :].rearrange("p (g t) -> p g t", g=H)[:, 8 * u + h2:8 * u + 8:2, :]
                    return nc.vector.tensor_tensor(o, src, bias.unsqueeze(2).to_broadcast([64, 4, HALF]), ALU.add)

                def q2_dst(u, h2, pp, src, bias):
                    o = qb[64 * pp:64 * pp + 64, :].rearrange("p (t e h) -> p t e h", e=2, h=H)[:, :, pp, 8 * u + h2:8 * u + 8:2]
                    return nc.vector.tensor_tensor(o, src.rearrange("p c t -> p t c"),
                                                   bias.unsqueeze(1).to_broadcast([64, HALF, 4]), ALU.add)

                def block_diagonal(ih):
                    o = pb[:, ih * 1024:(ih + 1) * 1024].rearrange("p (q k h) -> p q k h", q=2 * J, k=K)
                    i = bank(ring(par, PT2))[:, ih * 128:(ih + 1) * 128].rearrange("p (q h) -> p q h", h=H)
                    nc.vector.tensor_tensor(o, i.unsqueeze(2).to_broadcast([128, 2 * J, K, H]),
                                            mask[:].unsqueeze(1).unsqueeze(3).to_broadcast([128, 2 * J, K, H]),
                                            ALU.mult).then_inc(pb_ready, 1)

                if a:
                    qk_out(0)
                if d:
                    s2v = s2[:].rearrange("p (i g) -> p i g", g=H)
                    dve.wait_ge(s2_ready, s - 1)
                    nc.vector.reduce_max(mx2[:], s2v, AX.X).then_inc(mx2_ready, 1)
                if a:
                    qk_out(1)
                    qk_out(2)
                if d:
                    dve.wait_ge(exp2_ready, s - 1)
                    nc.vector.reduce_sum(sum2[:], s2v, AX.X).then_inc(sum2_ready, 1)
                if a:
                    qk_out(3)
                if d:
                    dve.wait_ge(sum2_ready, s - 1)
                    nc.vector.reciprocal(inv2[:], sum2[:]).then_inc(inv2_ready, 1)
                if bc:
                    if isinstance(s, int) and s == 1:
                        dve.wait_ge(in_bv, 16)
                    for u in range(2):
                        dve.wait_ge(mm_pv, 2 * s - 2 + u + 1)
                        nc.vector.tensor_tensor(ot[:, u * BANK:(u + 1) * BANK].rearrange("p (c t) -> p c t", c=4),
                                                bank(PV_BANK[u]).rearrange("p (c t) -> p c t", c=4),
                                                bv[:, 4 * u:4 * u + 4].unsqueeze(2).to_broadcast([128, 4, T]),
                                                ALU.add).then_inc(ot_ready, 1)
                    dve.wait_ge(mm_o, s)
                    dve.wait_ge(xres_ready, s)
                    nc.vector.tensor_tensor(t1[:], bank(ring(par, O), D), xres[b_par][:], ALU.add).then_inc(sum1_ready, 1)
                    dve.wait_ge(sum1_ready, s)
                    nc.vector.bn_stats(st1[:], t1[:]).then_inc(stats1_ready, 1)
                    dve.wait_ge(bq_scaled, 1)
                    dve.wait_ge(stats1_ready, s)
                    nc.vector.bn_aggr(mv1[:], st1[:]).then_inc(mv1_ready, 1)
                if d:
                    if isinstance(s, int) and s == LAST:
                        pass
                    dve.wait_ge(in_mask, 16)
                    dve.wait_ge(mm_pt2, s - 1)
                    block_diagonal(0)
                if bc:
                    dve.wait_ge(rs1_ready, s)
                    nc.vector.tensor_scalar(x1[:], t1[:], mv1[:, 0:1], rs1[:, 0:1], ALU.subtract, ALU.mult).then_inc(x1_ready, 1)
                if d:
                    block_diagonal(1)
                if a:
                    for q in range(4):
                        first = 8 * (q // 2) + q % 2
                        dve.wait_ge(mm_s, 4 * s + q + 1)
                        nc.vector.reduce_max(neg_max[:, first:first + 7:2], bank(S_BANK[q]).rearrange("p (h k) -> p h k", h=4),
                                             AX.X, negate=True).then_inc(max_ready, 1)
                    dve.wait_ge(exp_ready, 4 * s + 2)
                    nc.vector.reciprocal(row_inv[:, 0:8], row_sum[:, 0:8]).then_inc(inv_ready, 1)
                if bc:
                    if isinstance(s, int) and s == 1:
                        dve.wait_ge(in_bqk2, 32)
                    for u in range(2):
                        dve.wait_ge(mm_k2, 2 * s - 2 + u + 1)
                        halves_out(K2, u, bk2, k2_dst).then_inc(k2_ready, 1)
                    if isinstance(s, int) and s == 1:
                        dve.wait_ge(zeroed, 1)
                    for u in range(2):
                        dve.wait_ge(mm_q2, 2 * s - 2 + u + 1)
                        halves_out(Q2, u, bq2, q2_dst).then_inc(q2_ready, 1)
                if a:
                    dve.wait_ge(exp_ready, 4 * s + 4)
                    nc.vector.reciprocal(row_inv[:, 8:16], row_sum[:, 8:16]).then_inc(inv_ready, 1)
                if d:
                    dve.wait_ge(mm_o2, s - 1)
                    dve.wait_ge(x1b_ready, s - 1)
                    nc.vector.tensor_tensor(t2[:], bank(ring(par, O2), D), x1b[par][:], ALU.add).then_inc(sum2x_ready, 1)
                    dve.wait_ge(sum2x_ready, s - 1)
                    nc.vector.bn_stats(st2[:], t2[:]).then_inc(stats2_ready, 1)
                    dve.wait_ge(bq_scaled, 1)
                    dve.wait_ge(stats2_ready, s - 1)
                    nc.vector.bn_aggr(mv2[:], st2[:]).then_inc(mv2_ready, 1)

                def v2_out(u):
                    dve.wait_ge(mm_v2, 2 * s - 2 + u + 1)
                    nc.vector.tensor_tensor(v2s[:, u * BANK:(u + 1) * BANK], bank(ring(par, V2 + u)),
                                            bv2_row[:, u * BANK:(u + 1) * BANK], ALU.add).then_inc(v2s_ready, 1)

                if bc:
                    if isinstance(s, int) and s == 1:
                        dve.wait_ge(in_bv2, 16)
                    v2_out(0)
                if d:
                    dve.wait_ge(rs2_ready, s - 1)
                    nc.vector.tensor_scalar(x2[:], t2[:], mv2[:, 0:1], rs2[:, 0:1], ALU.subtract, ALU.mult).then_inc(x2_ready, 1)
                    dve.wait_ge(x2_ready, s - 1)
                    nc.vector.tensor_tensor_reduce(out=sq[:], in0=x2[:], in1=x2[:], scale=1.0, scalar=0.0,
                                                   op0=ALU.mult, op1=ALU.add, accum_out=ss[:, 0:1]).then_inc(ss_ready, 1)
                if bc:
                    v2_out(1)
                if d:
                    dve.wait_ge(ss_ready, s - 1)
                    nc.vector.tensor_scalar(ssm[:], ss[:], 1e-24, None, ALU.max).then_inc(ssm_ready, 1)
                if isinstance(s, int) and s == 1:
                    dve.wait_ge(in_ffn, 8 * 16)
                    nc.vector.tensor_scalar(wup[:, 0:FH], wup[:, 0:FH], gam[:, 1:2], D ** 0.5, ALU.mult, ALU.mult).then_inc(wup_scaled, 1)
                    nc.vector.tensor_scalar(wup[:, FH:FH + FL], wup[:, FH:FH + FL], gam[:, 0:1], D ** 0.5, ALU.mult, ALU.mult).then_inc(wup_scaled, 1)

            run_steps(dve, step)
            dve.wait_ge(x2b_ready, B)
            nc.vector.memset(scratch[:], 0.0).then_inc(y_banks_free, 1)
            with dve.Fori(0, B // GB) as g:
                t3v = t3[:].rearrange("p (b d) -> p b d", b=GB)
                dve.wait_ge(mm_y, g + 1)
                nc.vector.tensor_tensor(t3v, bank(4, BANK, 4).rearrange("p (b c) -> p b c", b=GB)[:, :, 0:D],
                                        x2b[:, bass.ds(g * (GB * D), GB * D)].rearrange("p (b d) -> p b d", b=GB),
                                        ALU.add).then_inc(y_banks_free, 1)
                dve.wait_ge(y_banks_free, g + 2)
                for bb in range(GB):
                    last = nc.vector.bn_stats(st3[:, 6 * bb:6 * bb + 6], t3v[:, bb, :])
                last.then_inc(stats3_ready, 1)
                dve.wait_ge(bq_scaled, 1)
                dve.wait_ge(stats3_ready, g + 1)
                for bb in range(GB):
                    last = nc.vector.bn_aggr(mv3[:, 2 * bb:2 * bb + 2], st3[:, 6 * bb:6 * bb + 6])
                last.then_inc(mv3_ready, 1)
                dve.wait_ge(rs3_ready, g + 1)
                for bb in range(GB):
                    last = nc.vector.tensor_scalar(x2b[:, bass.ds(g * (GB * D) + bb * D, D)], t3v[:, bb, :], mv3[:, 2 * bb:2 * bb + 1],
                                                   rs3[:, bb:bb + 1], ALU.subtract, ALU.mult)
                last.then_inc(out_ready, 1)
                dve.wait_ge(out_ready, g + 1)

        @block.tensor
        def _(pe):
            def step(s, h, par, a, bc, d, load):
                b_par = 1 - par
                static = isinstance(s, int)

                def project_qk(u):
                    if static and s == 0:
                        pe.wait_ge(in_wqk[u], 16)
                    if u == 0:
                        pe.wait_ge(in_xt[par], 16 * (h + 1))
                    if bc and d:
                        if u < 2:
                            pe.wait_ge(v2s_ready, 2 * s - 4 + u + 1)
                        elif u == 2:
                            pe.wait_ge(s2_ready, s - 1)
                    o = bank(ring(par, QK + u))
                    for c in range(4):
                        last = nc.tensor.matmul(o[:, c * T:(c + 1) * T], wqk[:, (4 * u + c) * 128:(4 * u + c + 1) * 128], xt[par][:],
                                                start=True, stop=True)
                    last.then_inc(mm_qk, 1)

                def transpose_p(u):
                    if static and s == 1 and u == 0:
                        pe.wait_ge(in_ident, 16)
                    if u % 2 == 0:
                        pe.wait_ge(p_ready, 2 * s - 2 + u // 2 + 1)
                    if u == 3:
                        pe.wait_ge(pt_ready, 4 * s - 4 + 1)
                    for i in range(4):
                        hd = 4 * u + i
                        last = nc.tensor.transpose(bank(T_BANK[u])[:, i * T:(i + 1) * T], p[:, hd * T:(hd + 1) * T], ident[:])
                    last.then_inc(mm_t, 1)

                if a:
                    project_qk(0)
                if bc:
                    transpose_p(0)
                    transpose_p(1)
                if a:
                    project_qk(1)
                if bc:
                    transpose_p(2)
                    transpose_p(3)
                if a:
                    project_qk(2)
                    project_qk(3)
                if bc:
                    for u in range(2):
                        pe.wait_ge(pt_ready, 4 * s - 4 + 2 * u + 2)
                        if u == 0:
                            pe.wait_ge(v_ready, 2 * s)
                        for i in range(8):
                            hd = 8 * u + i
                            last = nc.tensor.matmul(bank(PV_BANK[u])[64 * (i % 2):64 * (i % 2) + 64, (i // 2) * T:(i // 2 + 1) * T],
                                                    v[:, hd * DH:(hd + 1) * DH], pt[:, hd * T:(hd + 1) * T], start=True, stop=True)
                        last.then_inc(mm_pv, 1)
                if a:
                    if static and s == 0:
                        pe.wait_ge(in_wv, 16)
                    for u in range(2):
                        nc.tensor.matmul(bank(V_BANK[u]), xt[par][:], wv[:, u * BANK:(u + 1) * BANK], start=True, stop=True).then_inc(mm_v, 1)
                if bc:
                    if static and s == 1:
                        pe.wait_ge(in_wo, 16)
                    if a:
                        pe.wait_ge(qk_ready, 4 * s + 1)
                    else:
                        pe.wait_ge(v2s_ready, 2 * s - 2)
                        pe.wait_ge(s2_ready, s - 1)
                    pe.wait_ge(ot_ready, 2 * s)
                    for c in range(NC):
                        last = nc.tensor.matmul(bank(ring(par, O), D), ot[:, c * T:(c + 1) * T], wo[:, c * D:(c + 1) * D],
                                                start=c == 0, stop=c == NC - 1)
                    last.then_inc(mm_o, 1)
                if d:
                    if a:
                        pe.wait_ge(qk_ready, 4 * s + 2)
                    if not bc:
                        pe.wait_ge(v2s_ready, 2 * B)
                    pe.wait_ge(p2_ready, s - 1)
                    for ih in range(IH):
                        last = nc.tensor.transpose(bank(ring(par, PT2))[:, ih * 128:(ih + 1) * 128], s2[:, ih * 128:(ih + 1) * 128], ident[:])
                    last.then_inc(mm_pt2, 1)
                if a:
                    pe.wait_ge(qk_ready, 4 * s + 4)
                    for q in range(4):
                        pass
                    if bc:
                        pe.wait_ge(ot_ready, 2 * s)
                    for half in range(2):
                        if half == 1:
                            pe.wait_ge(v_ready, 2 * s + 2)
                        for i in range(8):
                            hd = 8 * half + i
                            rows = slice(64 * (i % 2), 64 * (i % 2) + 64)
                            cols = slice((hd // 2) * T, (hd // 2 + 1) * T)
                            mm = nc.tensor.matmul(bank(S_BANK[2 * half + i % 2])[:, (i // 2) * T:(i // 2 + 1) * T],
                                                  qt[rows, cols], kt[rows, cols], start=True, stop=True)
                            if i >= 6:
                                mm.then_inc(mm_s, 1)
                if bc:
                    if static and s == 1:
                        pe.wait_ge(in_perm, 16)
                    pe.wait_ge(x1_ready, s)
                    nc.tensor.transpose(bank(ring(par, X1T), T), x1[:], perm[:]).then_inc(mm_x1t, 1)
                if d:
                    pe.wait_ge(v2_moved, 16 * 16 * (s - 1))
                    for ih in range(IH):
                        if ih == 1 and bc:
                            pe.wait_ge(sum1_ready, s)
                        pe.wait_ge(pb_ready, 2 * (s - 2) + ih + 1)
                        for q in range(2 * J):
                            pp = q % 2
                            last = nc.tensor.matmul(bank(ring(par, PV2 + ih))[64 * pp:64 * pp + 64, (q // 2) * 128:(q // 2 + 1) * 128],
                                                    v2[:, (q * IH + ih) * DH:(q * IH + ih + 1) * DH],
                                                    pb[:, (ih * 2 * J + q) * 128:(ih * 2 * J + q + 1) * 128], start=True, stop=True)
                        last.then_inc(mm_pv2, 1)
                if bc:
                    if static and s == 1:
                        pe.wait_ge(in_wk2, 16)
                    pe.wait_ge(in_ct[b_par], 16 * (h + 1 if par == 1 else h))
                    for u in range(2):
                        if u == 0 and d:
                            pe.wait_ge(pb_ready, 2 * (s - 2) + 2)
                        if u == 1:
                            pe.wait_ge(x1t_ready, s)
                        for c in range(4):
                            last = nc.tensor.matmul(bank(ring(par, K2 + u))[:, c * T:(c + 1) * T],
                                                    wk2[:, (4 * u + c) * 128:(4 * u + c + 1) * 128], ct[b_par][:], start=True, stop=True)
                        last.then_inc(mm_k2, 1)
                    if static and s == 1:
                        pe.wait_ge(in_wq2, 16)
                    for u in range(2):
                        if d:
                            pe.wait_ge(ot2_ready, 2 * (s - 2) + u + 1)
                        for c in range(4):
                            last = nc.tensor.matmul(bank(ring(par, Q2 + u))[:, c * T:(c + 1) * T],
                                                    wq2[:, (4 * u + c) * 128:(4 * u + c + 1) * 128], x1t[:], start=True, stop=True)
                        last.then_inc(mm_q2, 1)
                if d:
                    if static and s == 2:
                        pass
                    pe.wait_ge(in_wo2, 16)
                    pe.wait_ge(ot2_ready, 2 * (s - 2) + 2)
                    if bc:
                        pe.wait_ge(k2_ready, 2 * s - 2 + 1)
                    for k in range(K):
                        last = nc.tensor.matmul(bank(ring(par, O2), D), ot2[:, k * 128:(k + 1) * 128], wo2[:, k * D:(k + 1) * D],
                                                start=k == 0, stop=k == K - 1)
                    last.then_inc(mm_o2, 1)
                if bc:
                    if static and s == 1:
                        pe.wait_ge(in_wv2, 16)
                    for u in range(2):
                        if u == 0:
                            pe.wait_ge(k2_ready, 2 * s)
                        else:
                            pe.wait_ge(q2_ready, 2 * s - 2 + 1)
                        nc.tensor.matmul(bank(ring(par, V2 + u)), ct[b_par][:], wv2[:, u * BANK:(u + 1) * BANK],
                                         start=True, stop=True).then_inc(mm_v2, 1)
                    pe.wait_ge(q2_ready, 2 * s)
                    for i in range(IH * K):
                        if i == 8 and d:
                            pe.wait_ge(sum2x_ready, s - 1)
                        last = nc.tensor.matmul(bank(ring(par, S2), BANK, 2)[:, i * H * J:(i + 1) * H * J],
                                                qb[:, i * 128:(i + 1) * 128],
                                                kt2[:].rearrange("p (g t) -> p g t", g=H)[:, :, J * i:J * i + J], start=True, stop=True)
                    last.then_inc(mm_s2, 1)
                if d:
                    if a:
                        pe.wait_ge(exp_ready, 4 * s + 4)
                    pe.wait_ge(xn_ready, s - 1)
                    nc.tensor.transpose(bank(X2T_BANK, T), xn[:], ident[:]).then_inc(mm_x2t, 1)

            run_steps(pe, step)

            pe.wait_ge(xnt_ready, B)
            pe.wait_ge(wup_scaled, 2)
            with pe.Fori(0, B // GB) as g:
                def up(c):
                    m = 128 if c < NF - 1 else FL
                    if c == NF - 1:
                        pe.wait_ge(wup_scaled, 2)
                        pe.wait_ge(ht_ready, NF * g + 1)
                    nc.tensor.matmul(bank(c % 4)[0:m, :], wup[:, c * 128:c * 128 + m], xnt[:, bass.ds(g * (GB * T), GB * T)],
                                     start=True, stop=True).then_inc(mm_h, 1)

                def down(c):
                    m = 128 if c < NF - 1 else FL
                    pe.wait_ge(ht_ready, NF * g + c + 1)
                    if c == 0:
                        pe.wait_ge(y_banks_free, g + 1)
                    for bb in range(GB):
                        w = wdn[:, c * D:(c + 1) * D] if c < NF - 1 else wdl[:]
                        last = nc.tensor.matmul(bank(4 + bb, D), ht[c][0:m, bb * T:(bb + 1) * T], w,
                                                start=c == 0, stop=c == NF - 1)
                    return last

                up(0)
                up(1)
                for c in range(NF):
                    last = down(c)
                    if c + 2 < NF:
                        up(c + 2)
                last.then_inc(mm_y, 1)


def kernel(x, ctx_1024, L0_attn_W_Q, L0_attn_b_Q, L0_attn_W_K, L0_attn_b_K, L0_attn_W_V, L0_attn_b_V, L0_attn_W_O,
           L0_attn_b_O, L0_xattn_Wq, L0_xattn_bq, L0_xattn_Wk, L0_xattn_bk, L0_xattn_Wv, L0_xattn_bv, L0_xattn_Wo,
           L0_xattn_bo, L0_ffn_routing_token, L0_ffn_light_gamma, L0_ffn_light_w1, L0_ffn_light_b1, L0_ffn_light_w2,
           L0_ffn_light_b2, L0_ffn_heavy_gamma, L0_ffn_heavy_w1, L0_ffn_heavy_b1, L0_ffn_heavy_w2, L0_ffn_heavy_b2):
    import numpy as np
    import concourse.bacc as bacc
    from concourse.bass_utils import run_bass_kernel_spmd

    def a(z):
        return np.ascontiguousarray(np.asarray(z))

    def chunks(z):
        return a(np.asarray(z).reshape(-1, 128).T)

    order = np.arange(T).reshape(IH, J, 2, K).transpose(2, 0, 3, 1).reshape(-1)
    perm = np.zeros((T, T), np.float32)
    perm[order, np.arange(T)] = 1.0
    mask = np.zeros((128, K), np.float32)
    mask[np.arange(128), np.arange(128) // H] = 1.0
    x = np.asarray(x)
    c = np.asarray(ctx_1024)
    b_up = np.zeros((128, NF), np.float32)
    b_up[:, 0:NF - 1] = np.asarray(L0_ffn_heavy_b1).reshape(NF - 1, 128).T
    b_up[0:FL, NF - 1] = np.asarray(L0_ffn_light_b1)
    arrays = {
        "x_nat": a(x),
        "x_t": a(x.transpose(0, 2, 1)),
        "ctx_t": a(c[:, order, :].transpose(0, 2, 1)),
        "w_qk": a(np.concatenate([np.asarray(L0_attn_W_Q).reshape(HD, D).T, np.asarray(L0_attn_W_K).reshape(HD, D).T], 1)),
        "w_v": a(np.asarray(L0_attn_W_V).reshape(HD, D).T),
        "w_o": a(np.asarray(L0_attn_W_O).transpose(0, 2, 1).reshape(NC, 128, D).transpose(1, 0, 2).reshape(128, NC * D)),
        "b_qk": a(np.concatenate([chunks(np.asarray(L0_attn_b_Q).reshape(-1)), chunks(np.asarray(L0_attn_b_K).reshape(-1))], 1)),
        "b_v": chunks(np.asarray(L0_attn_b_V).reshape(-1)),
        "b_o": a(L0_attn_b_O),
        "w2_q": a(np.asarray(L0_xattn_Wq).T),
        "w2_k": a(np.asarray(L0_xattn_Wk).T),
        "w2_v": a(np.asarray(L0_xattn_Wv).T),
        "w2_o": a(np.asarray(L0_xattn_Wo).reshape(D, 2, K, DH).transpose(1, 3, 2, 0).reshape(128, K * D)),
        "b2_q": chunks(L0_xattn_bq),
        "b2_k": chunks(L0_xattn_bk),
        "b2_v": a(L0_xattn_bv),
        "b2_o": a(L0_xattn_bo),
        "w_up": a(np.concatenate([np.asarray(L0_ffn_heavy_w1), np.asarray(L0_ffn_light_w1)], 1)),
        "g_light": a(np.asarray(L0_ffn_light_gamma).reshape(D, 1)),
        "g_heavy": a(np.asarray(L0_ffn_heavy_gamma).reshape(D, 1)),
        "w_down": a(np.asarray(L0_ffn_heavy_w2).reshape(NF - 1, 128, D).transpose(1, 0, 2).reshape(128, (NF - 1) * D)),
        "w_down_light": a(L0_ffn_light_w2),
        "b_up": b_up,
        "bd_light": a(L0_ffn_light_b2),
        "bd_heavy": a(L0_ffn_heavy_b2),
        "ident_in": np.eye(128, dtype=np.float32),
        "perm_in": perm,
        "mask_in": mask,
    }
    nc = bacc.Bacc("TRN2", target_bir_lowering=False, num_devices=1)
    args = {n: nc.dram_tensor(n, z.shape, mybir.dt.from_np(z.dtype), kind="ExternalInput").ap() for n, z in arrays.items()}
    out = nc.dram_tensor("out", (B, T, D), mybir.dt.float32, kind="ExternalOutput").ap()
    build(nc, out=out, **args)
    r = run_bass_kernel_spmd(nc, [arrays], core_ids=[0])
    return r.results[0]["out"]
```

```python
from contextlib import ExitStack

import concourse.bass as bass
from concourse import mybir

B, T, D = 16, 128, 128
H, DH = 16, 64
HD = H * DH
NC = HD // 128
HALF = T // 2
IH, J, K = 2, 4, 8
FH, FL = 512, 64
NF = FH // 128 + 1
GB = 4
BANK = 512
EPS = 1e-5
NG = B // GB


def build(nc, x_nat, x_t, ctx_t, w_qk, w_v, w_o, b_qk, b_v, b_o,
          w2_q, w2_k, w2_v, w2_o, b2_q, b2_k, b2_v, b2_o,
          w_up, g_light, g_heavy, w_down, w_down_light, b_up, bd_light, bd_heavy,
          ident_in, perm_in, mask_in, out):
    fp32 = mybir.dt.float32
    fp32r = mybir.dt.float32r
    ALU = mybir.AluOpType
    ACT = mybir.ActivationFunctionType
    AX = mybir.AxisListType

    ctx = ExitStack()
    with ctx:
        def sb(name, shape, dtype=fp32):
            return ctx.enter_context(nc.sbuf_tensor(name, shape, dtype))

        def sem(name):
            return ctx.enter_context(nc.semaphore(name))

        wqk_hi, wqk_lo = (sb("wqk_" + part, [128, 2 * HD], fp32r) for part in ("hi", "lo"))
        wv_hi, wv_lo = (sb("wv_" + part, [128, HD], fp32r) for part in ("hi", "lo"))
        wk2_hi, wk2_lo = (sb("wk2_" + part, [128, HD], fp32r) for part in ("hi", "lo"))
        wv2_hi, wv2_lo = (sb("wv2_" + part, [128, HD], fp32r) for part in ("hi", "lo"))
        wo = sb("wo", [128, NC * D])
        wq2 = sb("wq2", [128, HD])
        wo2 = sb("wo2", [128, K * D])
        wup = sb("wup", [128, FH + FL])
        wdn = sb("wdn", [128, (NF - 1) * D])
        wdl = sb("wdl", [FL, D])
        bqk = sb("bqk", [128, 2 * NC])
        bv = sb("bv", [128, NC])
        bo_row = sb("bo_row", [128, D])
        bq2 = sb("bq2", [128, NC])
        bk2 = sb("bk2", [128, NC])
        bv2_row = sb("bv2_row", [128, HD])
        bo2_row = sb("bo2_row", [128, D])
        bup = sb("bup", [128, NF])
        bdl_row = sb("bdl_row", [128, D])
        bdh_row = sb("bdh_row", [128, D])
        gam = sb("gam", [128, 2])
        ident = sb("ident", [128, 128])
        perm = sb("perm", [128, 128])
        mask = sb("mask", [128, K])
        minus_half = sb("minus_half", [128, 4])
        eps = sb("eps", [128, 4])

        xg, xg_hi, xg_lo = sb("xg", [128, GB * T]), sb("xg_hi", [128, GB * T], fp32r), sb("xg_lo", [128, GB * T], fp32r)
        cg, cg_hi, cg_lo = sb("cg", [128, GB * T]), sb("cg_hi", [128, GB * T], fp32r), sb("cg_lo", [128, GB * T], fp32r)
        xres = [sb(f"xres{i}", [T, D]) for i in range(2)]
        qt = sb("qt", [128, NC * GB * T])
        kt = sb("kt", [128, NC * GB * T])
        v = [sb(f"v{i}", [T, HD]) for i in range(2)]
        p = sb("p", [T, H * T])
        neg_max = sb("neg_max", [T, H])
        row_sum = sb("row_sum", [T, H])
        row_inv = sb("row_inv", [T, H])
        pt = sb("pt", [T, H * T])
        ot = sb("ot", [128, NC * T])
        t1 = sb("t1", [T, D])
        st1 = sb("st1", [T, 6])
        mv1 = sb("mv1", [T, 2])
        ve1 = sb("ve1", [T, 1])
        rs1 = sb("rs1", [T, 1])
        x1 = sb("x1", [T, D])
        x1b = [sb(f"x1b{i}", [T, D]) for i in range(2)]
        x1t = sb("x1t", [128, T])
        qb = sb("qb", [128, HALF * 2 * H])
        kt2 = sb("kt2", [128, GB * H * HALF])
        v2s = sb("v2s", [T, HD])
        v2 = sb("v2", [128, J * 2 * IH * DH])
        s2 = sb("s2", [128, IH * K * H])
        mx2 = sb("mx2", [128, IH * K])
        sum2 = sb("sum2", [128, IH * K])
        inv2 = sb("inv2", [128, IH * K])
        pb = sb("pb", [128, IH * J * 2 * K * H])
        ot2 = sb("ot2", [128, K * H * 8])
        t2 = sb("t2", [T, D])
        st2 = sb("st2", [T, 6])
        mv2 = sb("mv2", [T, 2])
        ve2 = sb("ve2", [T, 1])
        rs2 = sb("rs2", [T, 1])
        x2 = sb("x2", [T, D])
        sq = sb("sq", [T, D])
        ss = sb("ss", [T, 1])
        ssm = sb("ssm", [T, 1])
        rn = sb("rn", [T, 1])
        xn = sb("xn", [T, D])
        x2b = sb("x2b", [T, B * D])
        xnt = sb("xnt", [128, B * T])
        ht = [qt[:, c * GB * T:(c + 1) * GB * T] for c in range(NF)]
        t3 = sb("t3", [T, GB * D])
        st3 = sb("st3", [T, GB * 6])
        mv3 = sb("mv3", [T, GB * 2])
        ve3 = sb("ve3", [T, GB])
        rs3 = sb("rs3", [T, GB])

        wqk, wv, wk2, wv2 = pb, pt, ot2, v2

        ps = ctx.enter_context(nc.psum_tensor("ps", [128, 8 * BANK], fp32))

        def bank(n, cols=BANK, banks=1):
            return ps[:, n * BANK:n * BANK + (banks - 1) * BANK + cols]

        T_BANK = [7, 0, 1, 6]
        V_BANK = [7, 0]
        PV_BANK = [1, 6]
        S_BANK = [7, 0, 1, 6]
        V2, O, PT2, X1T, PV2, Q2, O2, S2 = [2, 3], 4, 5, 2, [3, 4], [5, 2], 3, 4
        BLOCK_BANKS = {"A": [3, 4, 5, 2], "B": [2, 3, 4, 5], "C": [2, 3, 4, 5], "D": [2, 3, 4, 5],
                       "E": [2, 3, 4, 5], "F": [2, 3, 4, 5]}

        def dve_count(group, blk, r):
            return 8 * group + 2 * "ABCD".index(blk) + r + 1

        def k2_dve_count(group, blk, r):
            return 4 * group + 2 * "EF".index(blk) + r + 1

        def k2_act_count(group, blk, r):
            return 4 * group + 2 * "EF".index(blk) + r - 1

        def k2_half(c, h2, pp, kt2, src):
            return (kt2[64 * pp:64 * pp + 64, :].rearrange("p (b g t) -> p b g t", b=GB, g=H)[:, :, 2 * c + h2, :],
                    src.rearrange("p (b e t) -> p b e t", b=GB, e=2)[64 * h2:64 * h2 + 64, :, pp, :])

        def ot2_half(ih):
            return (ot2[:].rearrange("p (k h e) -> p k h e", k=K, h=H)[:, :, :, ih * J:(ih + 1) * J].rearrange("p k h j -> p j k h"),
                    bank(PV2[ih]).rearrange("p (j k h) -> p j k h", j=J, k=K))

        def act_count(group, blk, r):
            return 8 * group + 2 * "ABCD".index(blk) + r - 1

        H_BANK, X2T_BANK, Y_BANK = [0, 1], 6, 7

        in_xres = [sem(f"in_xres{i}") for i in range(2)]
        in_xg, in_cg = sem("in_xg"), sem("in_cg")
        in_wqk = [sem(f"in_wqk{i}") for i in range(4)]
        in_bqk = sem("in_bqk")
        in_wv = sem("in_wv")
        in_ident = sem("in_ident")
        in_bv = sem("in_bv")
        in_wo = sem("in_wo")
        in_bo = sem("in_bo")
        in_perm = sem("in_perm")
        in_wk2 = sem("in_wk2")
        in_wq2 = sem("in_wq2")
        in_bqk2 = sem("in_bqk2")
        in_wv2 = sem("in_wv2")
        in_bv2 = sem("in_bv2")
        in_mask = sem("in_mask")
        in_wo2 = sem("in_wo2")
        in_bo2 = sem("in_bo2")
        in_ffn = sem("in_ffn")
        v2_moved = sem("v2_moved")
        out_stored = sem("out_stored")
        x_hi, x_lo, c_hi, c_lo, w_hi, w_lo = (sem(n) for n in ("x_hi", "x_lo", "c_hi", "c_lo", "w_hi", "w_lo"))
        mm_qk, mm_v, mm_s, mm_t, mm_pv, mm_o = (sem(n) for n in ("mm_qk", "mm_v", "mm_s", "mm_t", "mm_pv", "mm_o"))
        mm_x1t, mm_k2, mm_q2, mm_v2, mm_s2 = (sem(n) for n in ("mm_x1t", "mm_k2", "mm_q2", "mm_v2", "mm_s2"))
        mm_pt2, mm_pv2, mm_o2, mm_x2t = (sem(n) for n in ("mm_pt2", "mm_pv2", "mm_o2", "mm_x2t"))
        mm_h, mm_y = sem("mm_h"), sem("mm_y")
        qk_by_dve, qk_by_act = sem("qk_by_dve"), sem("qk_by_act")
        v_ready, max_ready, exp_ready = (sem(n) for n in ("v_ready", "max_ready", "exp_ready"))
        inv_ready, p_ready, pt_ready, ot_ready = (sem(n) for n in ("inv_ready", "p_ready", "pt_ready", "ot_ready"))
        xres_ready, sum1_ready, stats1_ready, mv1_ready = (sem(n) for n in ("xres_ready", "sum1_ready", "stats1_ready", "mv1_ready"))
        ve1_ready, rs1_ready, x1_ready, x1b_ready, x1t_ready = (sem(n) for n in ("ve1_ready", "rs1_ready", "x1_ready", "x1b_ready", "x1t_ready"))
        k2_by_dve, k2_by_act = sem("k2_by_dve"), sem("k2_by_act")
        q2_ready, v2s_ready, s2_ready = (sem(n) for n in ("q2_ready", "v2s_ready", "s2_ready"))
        mx2_ready, sub2_ready, exp2_ready, sum2_ready, inv2_ready, p2_ready = (
            sem(n) for n in ("mx2_ready", "sub2_ready", "exp2_ready", "sum2_ready", "inv2_ready", "p2_ready"))
        pb_ready, ot2_by_act, ot2_by_dve = sem("pb_ready"), sem("ot2_by_act"), sem("ot2_by_dve")
        sum2x_ready, stats2_ready, mv2_ready, ve2_ready, rs2_ready = (
            sem(n) for n in ("sum2x_ready", "stats2_ready", "mv2_ready", "ve2_ready", "rs2_ready"))
        x2_ready, ss_ready, ssm_ready, rn_ready, xn_ready, xnt_ready, x2b_ready = (
            sem(n) for n in ("x2_ready", "ss_ready", "ssm_ready", "rn_ready", "xn_ready", "xnt_ready", "x2b_ready"))
        zeroed, half_set, bq_scaled, wup_scaled, bd_summed = (sem(n) for n in ("zeroed", "half_set", "bq_scaled", "wup_scaled", "bd_summed"))
        ht_ready, y_read, stats3_ready, mv3_ready, ve3_ready, rs3_ready, out_ready = (
            sem(n) for n in ("ht_ready", "y_read", "stats3_ready", "mv3_ready", "ve3_ready", "rs3_ready", "out_ready"))

        block = ctx.enter_context(nc.Block())

        FIRST_LOOPED, LAST_LOOPED, LAST = 3, 14, B + 1

        def run_steps(eng, step):
            for s in range(FIRST_LOOPED):
                step(s, s // 2, s // GB, s % GB, s < B, 1 <= s <= B, s >= 2)
            with eng.Fori(0, (LAST_LOOPED + 1 - FIRST_LOOPED) // GB) as i:
                for n in range(FIRST_LOOPED, FIRST_LOOPED + GB):
                    step(GB * i + n, GB // 2 * i + n // 2, i + n // GB, n % GB, True, True, True)
            for s in range(LAST_LOOPED + 1, LAST):
                step(s, s // 2, s // GB, s % GB, s < B, 1 <= s <= B, s >= 2)

        SPLITS = ([(wqk, wqk_hi, wqk_lo, u, in_wqk[u]) for u in range(4)] + [(wv, wv_hi, wv_lo, u, in_wv) for u in range(2)] +
                  [(wk2, wk2_hi, wk2_lo, u, in_wk2) for u in range(2)] + [(wv2, wv2_hi, wv2_lo, u, in_wv2) for u in range(2)])
        WQK_SPLIT, WV_SPLIT, WK2_SPLIT, WV2_SPLIT = [1, 2, 3, 4], 6, 8, 10

        @block.sync
        def _(sp):
            sp.dma_start(xg[:], x_t[0]).then_inc(in_xg, 16)
            for u in range(4):
                sp.dma_start(wqk[:, u * BANK:(u + 1) * BANK], w_qk[:, u * BANK:(u + 1) * BANK]).then_inc(in_wqk[u], 16)
            sp.dma_start(wv[:, 0:HD], w_v).then_inc(in_wv, 16)
            sp.dma_start(cg[:], ctx_t[0]).then_inc(in_cg, 16)
            for tile, src, s_in in ((wk2[:], w2_k, in_wk2), (bk2[:], b2_k, in_bqk2), (bq2[:], b2_q, in_bqk2),
                                    (ident[:], ident_in, in_ident), (wv2[:], w2_v, in_wv2), (bv[:], b_v, in_bv),
                                    (wo[:], w_o, in_wo), (perm[:], perm_in, in_perm), (wq2[:], w2_q, in_wq2),
                                    (xres[1][:], x_nat[1], in_xres[1]), (mask[:], mask_in, in_mask), (wo2[:], w2_o, in_wo2)):
                sp.dma_start(tile, src).then_inc(s_in, 16)

            def step(s, h, g, phase, a, bc, d):
                b_par = 1 - phase % 2
                if phase == 3 and not isinstance(s, int):
                    sp.wait_ge(x_lo, g + 1)
                    sp.dma_start(xg[:], x_t[bass.ds(g + 1, 1)].rearrange("g p t -> p (g t)")).then_inc(in_xg, 16)
                    sp.wait_ge(c_lo, g + 1)
                    sp.dma_start(cg[:], ctx_t[bass.ds(g + 1, 1)].rearrange("g p t -> p (g t)")).then_inc(in_cg, 16)
                if a and bc and not (isinstance(s, int) and s == B - 1):
                    sp.wait_ge(sum1_ready, s)
                    sp.dma_start(xres[b_par][:], x_nat[bass.ds(s + 1, 1)].rearrange("b p t -> p (b t)")).then_inc(in_xres[b_par], 16)
                if bc:
                    if d:
                        sp.wait_ge(mm_pv2, 2 * s - 2)
                    else:
                        sp.wait_ge(v2s_ready, 2 * s)
                    for j in range(J):
                        for pp in range(2):
                            for ih in range(IH):
                                first = pp * HALF + ih * K * J + j
                                col = ((j * 2 + pp) * IH + ih) * DH
                                sp.dma_start(v2[:, col:col + DH],
                                             v2s[first:first + (K - 1) * J + 1:J, :].rearrange("k (g d) -> k g d", g=H)
                                             ).then_inc(v2_moved, 16)

            run_steps(sp, step)
            with sp.Fori(0, B // GB) as g:
                sp.wait_ge(out_ready, g + 1)
                sp.dma_start(out[bass.ds(g * GB, GB)].rearrange("b t d -> t b d"),
                             x2b[:, bass.ds(g * (GB * D), GB * D)].rearrange("t (b d) -> t b d", b=GB)
                             ).then_inc(out_stored, 16)
            sp.wait_ge(out_stored, 16 * (B // GB))

        @block.gpsimd
        def _(pool):
            nc.gpsimd.memset(minus_half[:], -0.5).then_inc(half_set, 1)
            nc.gpsimd.memset(eps[:], EPS).then_inc(half_set, 1)
            nc.gpsimd.memset(qb[:], 0.0).then_inc(zeroed, 1)
            pool.dma_start(bo_row[:], b_o.partition_broadcast(128)).then_inc(in_bo, 16)
            pool.dma_start(bo2_row[:], b2_o.partition_broadcast(128)).then_inc(in_bo2, 16)
            pool.dma_start(bv2_row[:], b2_v.partition_broadcast(128)).then_inc(in_bv2, 16)
            for tile, src in ((bdl_row[:], bd_light.partition_broadcast(128)), (bdh_row[:], bd_heavy.partition_broadcast(128)),
                              (gam[:, 0:1], g_light), (gam[:, 1:2], g_heavy), (wup[:], w_up),
                              (wdn[:], w_down), (wdl[:], w_down_light), (bup[:], b_up)):
                pool.dma_start(tile, src).then_inc(in_ffn, 16)
            pool.wait_ge(in_bo, 16)
            pool.wait_ge(in_ffn, 8 * 16)
            nc.gpsimd.tensor_tensor(bdl_row[:], bdl_row[:], bdh_row[:], ALU.add).then_inc(bd_summed, 1)
            pool.wait_ge(bd_summed, 1)
            pool.wait_ge(half_set, 2)
            pool.wait_ge(in_bo2, 16)
            s2v = s2[:].rearrange("p (i g) -> p i g", g=H)

            def softmax2(s):
                pool.wait_ge(mx2_ready, s - 1)
                nc.gpsimd.tensor_tensor(s2v, s2v, mx2[:].unsqueeze(2).to_broadcast([128, IH * K, H]),
                                        ALU.subtract).then_inc(sub2_ready, 1)
                pool.wait_ge(inv2_ready, s - 1)
                nc.gpsimd.tensor_tensor(s2v, s2v, inv2[:].unsqueeze(2).to_broadcast([128, IH * K, H]),
                                        ALU.mult).then_inc(p2_ready, 1)

            def rstd2(s):
                pool.wait_ge(mv2_ready, s - 1)
                nc.gpsimd.tensor_tensor(ve2[:], mv2[:, 1:2], eps[:, 0:1], ALU.add).then_inc(ve2_ready, 1)
                pool.wait_ge(ve2_ready, s - 1)
                nc.gpsimd.tensor_tensor(rs2[:], ve2[:], minus_half[:, 0:1], ALU.pow).then_inc(rs2_ready, 1)

            def rms2(s):
                pool.wait_ge(ssm_ready, s - 1)
                nc.gpsimd.tensor_tensor(rn[:], ssm[:], minus_half[:, 0:1], ALU.pow).then_inc(rn_ready, 1)
                nc.gpsimd.tensor_tensor(x2b[:, bass.ds((s - 2) * D, D)], x2[:], bdl_row[:], ALU.add).then_inc(x2b_ready, 1)

            def step(s, h, g, phase, a, bc, d):
                par, b_par = phase % 2, 1 - phase % 2
                if a:
                    pool.wait_ge(in_xres[par], 16 * (h + 1))
                    nc.gpsimd.tensor_tensor(xres[par][:], xres[par][:], bo_row[:], ALU.add).then_inc(xres_ready, 1)
                if d:
                    softmax2(s)
                if bc:
                    pool.wait_ge(mv1_ready, s)
                    nc.gpsimd.tensor_tensor(ve1[:], mv1[:, 1:2], eps[:, 0:1], ALU.add).then_inc(ve1_ready, 1)
                    pool.wait_ge(ve1_ready, s)
                    nc.gpsimd.tensor_tensor(rs1[:], ve1[:], minus_half[:, 0:1], ALU.pow).then_inc(rs1_ready, 1)
                    pool.wait_ge(x1_ready, s)
                    nc.gpsimd.tensor_tensor(x1b[b_par][:], x1[:], bo2_row[:], ALU.add).then_inc(x1b_ready, 1)
                for half in range(2):
                    if a:
                        pool.wait_ge(inv_ready, 2 * s + half + 1)
                        ph = p[:, half * 8 * T:(half + 1) * 8 * T].rearrange("q (h k) -> q h k", h=8)
                        nc.gpsimd.tensor_tensor(ph, ph, row_inv[:, 8 * half:8 * half + 8].unsqueeze(2).to_broadcast([T, 8, T]),
                                                ALU.mult).then_inc(p_ready, 1)
                if d:
                    rstd2(s)
                    rms2(s)

            run_steps(pool, step)
            for g in range(B // GB):
                if g == 0:
                    softmax2(LAST)
                if g == 1:
                    rstd2(LAST)
                    rms2(LAST)
                pool.wait_ge(mv3_ready, g + 1)
                nc.gpsimd.tensor_tensor(ve3[:], mv3[:].rearrange("p (b m) -> p b m", m=2)[:, :, 1], eps[:], ALU.add).then_inc(ve3_ready, 1)
                pool.wait_ge(ve3_ready, g + 1)
                nc.gpsimd.tensor_tensor(rs3[:], ve3[:], minus_half[:], ALU.pow).then_inc(rs3_ready, 1)

        @block.scalar
        def _(act):
            act.dma_start(bqk[:], b_qk).then_inc(in_bqk, 16)
            act.dma_start(xres[0][:], x_nat[0]).then_inc(in_xres[0], 16)

            def split_hi(n):
                tile, hi, _, u, loaded = SPLITS[n]
                act.wait_ge(loaded, 16)
                nc.scalar.activation(hi[:, u * BANK:(u + 1) * BANK], tile[:, u * BANK:(u + 1) * BANK], ACT.Copy).then_inc(w_hi, 1)

            def x_high(group):
                act.wait_ge(in_xg, 16 * group + 16)
                nc.scalar.activation(xg_hi[:], xg[:], ACT.Copy).then_inc(x_hi, 1)

            def c_high(group):
                act.wait_ge(in_cg, 16 * group + 16)
                nc.scalar.activation(cg_hi[:], cg[:], ACT.Copy).then_inc(c_hi, 1)

            def qk_out(group, blk):
                for r in (2, 3):
                    u = 4 * "ABCD".index(blk) + r
                    dst = (qt if u < NC else kt)[:, (u % NC) * GB * T:(u % NC + 1) * GB * T]
                    act.wait_ge(mm_qk, 16 * group + u + 1)
                    nc.scalar.activation(dst, bank(BLOCK_BANKS[blk][r]), ACT.Identity, bias=bqk[:, u:u + 1],
                                         scale=DH ** -0.5 if u < NC else 1.0).then_inc(qk_by_act, 1)

            def k2_out(group, blk):
                for r in (2, 3):
                    c = 4 * "EF".index(blk) + r
                    act.wait_ge(mm_k2, 8 * group + c + 1)
                    for h2 in range(2):
                        for pp in range(2):
                            dst, src = k2_half(c, h2, pp, kt2, bank(BLOCK_BANKS[blk][r]))
                            last = nc.scalar.activation(dst, src, ACT.Identity, bias=bk2[64 * h2:64 * h2 + 64, c:c + 1])
                    last.then_inc(k2_by_act, 1)

            def exp2(s):
                act.wait_ge(sub2_ready, s - 1)
                nc.scalar.activation(s2[:], s2[:], ACT.Exp, scale=DH ** -0.5).then_inc(exp2_ready, 1)

            def regrouped(s):
                act.wait_ge(mm_pv2, 2 * (s - 2) + 1)
                dst, src = ot2_half(0)
                nc.scalar.activation(dst, src, ACT.Copy).then_inc(ot2_by_act, 1)

            def normed_x2(s):
                act.wait_ge(rn_ready, s - 1)
                nc.scalar.activation(xn[:], x2[:], ACT.Copy, scale=rn[:, 0:1]).then_inc(xn_ready, 1)

            def x2_transposed(s, where):
                act.wait_ge(mm_x2t, s - 1)
                nc.scalar.activation(xnt[:, bass.ds((s - 2) * T, T)], bank(where, T), ACT.Copy).then_inc(xnt_ready, 1)

            def step(s, h, g, phase, a, bc, d):
                par, b_par = phase % 2, 1 - phase % 2

                def transposed(u):
                    act.wait_ge(mm_t, 4 * s - 4 + u + 1)
                    nc.scalar.activation(pt[:, u * BANK:(u + 1) * BANK], bank(T_BANK[u]), ACT.Copy).then_inc(pt_ready, 1)

                def exponentials(q):
                    act.wait_ge(max_ready, 4 * s + q + 1)
                    for pos in range(4):
                        hd = 8 * (q // 2) + 2 * pos + q % 2
                        last = nc.scalar.activation(p[:, hd * T:(hd + 1) * T], bank(S_BANK[q])[:, pos * T:(pos + 1) * T], ACT.Exp,
                                                    bias=neg_max[:, hd:hd + 1], accum_out=row_sum[:, hd:hd + 1])
                    last.then_inc(exp_ready, 1)

                static = isinstance(s, int)
                if static and s == 0:
                    x_high(0)
                    split_hi(0)
                    split_hi(1)
                    split_hi(2)
                    act.wait_ge(bq_scaled, 1)
                    qk_out(0, "A")
                    split_hi(3)
                    qk_out(0, "B")
                    split_hi(4)
                    split_hi(5)
                if bc:
                    transposed(0)
                    transposed(1)
                if phase == 0 and a:
                    qk_out(g, "C")
                if bc:
                    transposed(2)
                    transposed(3)
                if d:
                    exp2(s)
                if phase == 0 and a:
                    qk_out(g, "D")
                if phase == 1 and a:
                    k2_out(g, "F")
                if a:
                    for u in range(2):
                        act.wait_ge(mm_v, 2 * s + u + 1)
                        nc.scalar.activation(v[par][:, u * BANK:(u + 1) * BANK], bank(V_BANK[u]), ACT.Copy).then_inc(v_ready, 1)
                if static and s == 0:
                    c_high(0)
                    split_hi(6)
                    split_hi(7)
                if not static or s > 2:
                    normed_x2(s - 1)
                    x2_transposed(s - 1, V_BANK[0])
                if a:
                    exponentials(0)
                if phase == 0 and bc and a:
                    act.wait_ge(mm_v2, 2 * s)
                    c_high(g)
                if bc:
                    act.wait_ge(mm_x1t, s)
                    nc.scalar.activation(x1t[:], bank(X1T, T), ACT.Copy).then_inc(x1t_ready, 1)
                if a:
                    exponentials(1)
                if phase == 3 and not static:
                    act.wait_ge(mm_v, 2 * s + 2)
                    x_high(g + 1)
                if d:
                    regrouped(s)
                if a:
                    exponentials(2)
                    exponentials(3)
                if phase == 3 and not static:
                    qk_out(g + 1, "A")
                if static and s == 0:
                    split_hi(8)
                    split_hi(9)
                if phase == 3 and not static:
                    qk_out(g + 1, "B")
                if phase == 0 and a:
                    if static and s == 0:
                        act.wait_ge(in_bqk2, 32)
                    k2_out(g, "E")

            run_steps(act, step)
            act.wait_ge(in_ffn, 8 * 16)
            for g in range(B // GB):
                for c in range(NF):
                    if (g, c) == (0, 0):
                        exp2(LAST)
                    if (g, c) == (0, 4):
                        normed_x2(LAST - 1)
                        x2_transposed(LAST - 1, X2T_BANK)
                    if (g, c) == (1, 2):
                        regrouped(LAST)
                    if (g, c) == (2, 3):
                        normed_x2(LAST)
                    if (g, c) == (2, 4):
                        x2_transposed(LAST, X2T_BANK)
                    m = 128 if c < NF - 1 else FL
                    act.wait_ge(mm_h, NF * g + c + 1)
                    nc.scalar.activation(ht[c][0:m, :], bank(H_BANK[(NF * g + c) % 2])[0:m, :], ACT.Gelu,
                                         bias=bup[0:m, c:c + 1]).then_inc(ht_ready, 1)

        @block.vector
        def _(dve):
            dve.wait_ge(in_bqk, 16)
            nc.vector.tensor_scalar(bqk[:, 0:NC], bqk[:, 0:NC], DH ** -0.5, None, ALU.mult).then_inc(bq_scaled, 1)
            dve.wait_ge(bq_scaled, 1)
            s2v = s2[:].rearrange("p (i g) -> p i g", g=H)

            def split_lo(n):
                tile, hi, lo, u, _ = SPLITS[n]
                cols = slice(u * BANK, (u + 1) * BANK)
                dve.wait_ge(w_hi, n + 1)
                nc.vector.tensor_tensor(lo[:, cols], tile[:, cols], hi[:, cols].bitcast(fp32), ALU.subtract).then_inc(w_lo, 1)

            def x_low(group):
                dve.wait_ge(x_hi, group + 1)
                nc.vector.tensor_tensor(xg_lo[:], xg[:], xg_hi[:].bitcast(fp32), ALU.subtract).then_inc(x_lo, 1)

            def c_low(group):
                dve.wait_ge(c_hi, group + 1)
                nc.vector.tensor_tensor(cg_lo[:], cg[:], cg_hi[:].bitcast(fp32), ALU.subtract).then_inc(c_lo, 1)

            def qk_out(group, blk):
                for r in (0, 1):
                    u = 4 * "ABCD".index(blk) + r
                    dst = (qt if u < NC else kt)[:, (u % NC) * GB * T:(u % NC + 1) * GB * T]
                    dve.wait_ge(mm_qk, 16 * group + u + 1)
                    nc.vector.tensor_scalar(dst, bank(BLOCK_BANKS[blk][r]), DH ** -0.5 if u < NC else 1.0, bqk[:, u:u + 1],
                                            ALU.mult, ALU.add).then_inc(qk_by_dve, 1)

            def k2_out(group, blk):
                for r in (0, 1):
                    c = 4 * "EF".index(blk) + r
                    dve.wait_ge(mm_k2, 8 * group + c + 1)
                    for h2 in range(2):
                        for pp in range(2):
                            dst, src = k2_half(c, h2, pp, kt2, bank(BLOCK_BANKS[blk][r]))
                            last = nc.vector.tensor_scalar(dst, src, bk2[64 * h2:64 * h2 + 64, c:c + 1], None, ALU.add)
                    last.then_inc(k2_by_dve, 1)

            def regrouped(s):
                dve.wait_ge(mm_pv2, 2 * (s - 2) + 2)
                dst, src = ot2_half(1)
                nc.vector.tensor_copy(dst, src).then_inc(ot2_by_dve, 1)

            def max2(s):
                dve.wait_ge(s2_ready, s - 1)
                nc.vector.reduce_max(mx2[:], s2v, AX.X).then_inc(mx2_ready, 1)

            def sums2(s):
                dve.wait_ge(exp2_ready, s - 1)
                nc.vector.reduce_sum(sum2[:], s2v, AX.X).then_inc(sum2_ready, 1)
                dve.wait_ge(sum2_ready, s - 1)
                nc.vector.reciprocal(inv2[:], sum2[:]).then_inc(inv2_ready, 1)

            def block_diagonal(s, ih):
                dve.wait_ge(mm_pt2, s - 1)
                o = pb[:, ih * 1024:(ih + 1) * 1024].rearrange("p (q k h) -> p q k h", q=2 * J, k=K)
                i = bank(PT2)[:, ih * 128:(ih + 1) * 128].rearrange("p (q h) -> p q h", h=H)
                nc.vector.tensor_tensor(o, i.unsqueeze(2).to_broadcast([128, 2 * J, K, H]),
                                        mask[:].unsqueeze(1).unsqueeze(3).to_broadcast([128, 2 * J, K, H]),
                                        ALU.mult).then_inc(pb_ready, 1)

            def stats2(s, par):
                dve.wait_ge(mm_o2, s - 1)
                dve.wait_ge(x1b_ready, s - 1)
                nc.vector.tensor_tensor(t2[:], bank(O2, D), x1b[par][:], ALU.add).then_inc(sum2x_ready, 1)
                dve.wait_ge(sum2x_ready, s - 1)
                nc.vector.bn_stats(st2[:], t2[:]).then_inc(stats2_ready, 1)
                dve.wait_ge(bq_scaled, 1)
                dve.wait_ge(stats2_ready, s - 1)
                nc.vector.bn_aggr(mv2[:], st2[:]).then_inc(mv2_ready, 1)

            def x2_out(s):
                dve.wait_ge(rs2_ready, s - 1)
                nc.vector.tensor_scalar(x2[:], t2[:], mv2[:, 0:1], rs2[:, 0:1], ALU.subtract, ALU.mult).then_inc(x2_ready, 1)
                dve.wait_ge(x2_ready, s - 1)
                nc.vector.tensor_tensor_reduce(out=sq[:], in0=x2[:], in1=x2[:], scale=1.0, scalar=0.0,
                                               op0=ALU.mult, op1=ALU.add, accum_out=ss[:, 0:1]).then_inc(ss_ready, 1)
                dve.wait_ge(ss_ready, s - 1)
                nc.vector.tensor_scalar(ssm[:], ss[:], 1e-24, None, ALU.max).then_inc(ssm_ready, 1)

            def step(s, h, g, phase, a, bc, d):
                par, b_par = phase % 2, 1 - phase % 2
                static = isinstance(s, int)

                def q2_out(u):
                    dve.wait_ge(mm_q2, 2 * s - 2 + u + 1)
                    src = bank(Q2[u]).rearrange("p (c e t) -> p c e t", c=4, e=2)
                    for h2 in range(2):
                        rows = slice(64 * h2, 64 * h2 + 64)
                        for pp in range(2):
                            o = qb[64 * pp:64 * pp + 64, :].rearrange("p (t e h) -> p t e h", e=2, h=H)[:, :, pp, 8 * u + h2:8 * u + 8:2]
                            last = nc.vector.tensor_tensor(o, src[rows, :, pp, :].rearrange("p c t -> p t c"),
                                                           bq2[rows, 4 * u:4 * u + 4].unsqueeze(1).to_broadcast([64, HALF, 4]), ALU.add)
                    last.then_inc(q2_ready, 1)

                def score_max(q):
                    first = 8 * (q // 2) + q % 2
                    dve.wait_ge(mm_s, 4 * s + q + 1)
                    nc.vector.reduce_max(neg_max[:, first:first + 7:2], bank(S_BANK[q]).rearrange("p (h k) -> p h k", h=4),
                                         AX.X, negate=True).then_inc(max_ready, 1)

                if static and s == 0:
                    x_low(0)
                    split_lo(0)
                    split_lo(1)
                    split_lo(2)
                    qk_out(0, "A")
                    split_lo(3)
                    qk_out(0, "B")
                    split_lo(4)
                    split_lo(5)
                if d:
                    max2(s)
                if phase == 0 and a:
                    qk_out(g, "C")
                if d:
                    sums2(s)
                if phase == 0 and a:
                    qk_out(g, "D")
                if phase == 1 and a:
                    k2_out(g, "F")
                if static and s == 0:
                    c_low(0)
                    split_lo(6)
                    split_lo(7)
                if bc:
                    if static and s == 1:
                        dve.wait_ge(in_bv, 16)
                    for u in range(2):
                        dve.wait_ge(mm_pv, 2 * s - 2 + u + 1)
                        nc.vector.tensor_tensor(ot[:, u * BANK:(u + 1) * BANK].rearrange("p (c t) -> p c t", c=4),
                                                bank(PV_BANK[u]).rearrange("p (c t) -> p c t", c=4),
                                                bv[:, 4 * u:4 * u + 4].unsqueeze(2).to_broadcast([128, 4, T]),
                                                ALU.add).then_inc(ot_ready, 1)
                    if static and s == 1:
                        dve.wait_ge(in_bv2, 16)
                    if d:
                        dve.wait_ge(v2_moved, 16 * 16 * (s - 1))
                    for u in range(2):
                        dve.wait_ge(mm_v2, 2 * s - 2 + u + 1)
                        nc.vector.tensor_tensor(v2s[:, u * BANK:(u + 1) * BANK], bank(V2[u]),
                                                bv2_row[:, u * BANK:(u + 1) * BANK], ALU.add).then_inc(v2s_ready, 1)
                    dve.wait_ge(mm_o, s)
                    dve.wait_ge(xres_ready, s)
                    nc.vector.tensor_tensor(t1[:], bank(O, D), xres[b_par][:], ALU.add).then_inc(sum1_ready, 1)
                    dve.wait_ge(sum1_ready, s)
                    nc.vector.bn_stats(st1[:], t1[:]).then_inc(stats1_ready, 1)
                    dve.wait_ge(bq_scaled, 1)
                    dve.wait_ge(stats1_ready, s)
                    nc.vector.bn_aggr(mv1[:], st1[:]).then_inc(mv1_ready, 1)
                if d:
                    dve.wait_ge(in_mask, 16)
                    block_diagonal(s, 0)
                if a:
                    score_max(0)
                if bc:
                    dve.wait_ge(rs1_ready, s)
                    nc.vector.tensor_scalar(x1[:], t1[:], mv1[:, 0:1], rs1[:, 0:1], ALU.subtract, ALU.mult).then_inc(x1_ready, 1)
                if a:
                    score_max(1)
                if d:
                    block_diagonal(s, 1)
                if a:
                    score_max(2)
                    score_max(3)
                if phase == 3 and not static:
                    x_low(g + 1)
                if phase == 0 and a and bc:
                    c_low(g)
                if bc:
                    if static and s == 1:
                        dve.wait_ge(zeroed, 1)
                        dve.wait_ge(in_bqk2, 32)
                    q2_out(0)
                if d:
                    regrouped(s)
                if a:
                    dve.wait_ge(exp_ready, 4 * s + 2)
                    nc.vector.reciprocal(row_inv[:, 0:8], row_sum[:, 0:8]).then_inc(inv_ready, 1)
                if bc:
                    q2_out(1)
                if phase == 3 and not static:
                    qk_out(g + 1, "A")
                if a:
                    dve.wait_ge(exp_ready, 4 * s + 4)
                    nc.vector.reciprocal(row_inv[:, 8:16], row_sum[:, 8:16]).then_inc(inv_ready, 1)
                if d:
                    stats2(s, par)
                if d:
                    x2_out(s)
                if bc:
                    dve.wait_ge(mm_s2, s)
                    sp2 = bank(S2, BANK, 2).rearrange("p (i g j) -> p i g j", g=H, j=J)
                    for j in range(J):
                        last = nc.vector.tensor_copy(s2[32 * j:32 * j + 32, :].rearrange("p (i g) -> p i g", g=H),
                                                    sp2[32 * j:32 * j + 32, :, :, j])
                    last.then_inc(s2_ready, 1)
                if static and s == 0:
                    split_lo(8)
                    split_lo(9)
                    dve.wait_ge(in_bqk2, 32)
                if phase == 0 and a:
                    k2_out(g, "E")
                if phase == 3 and not static:
                    qk_out(g + 1, "B")
                if static and s == 1:
                    dve.wait_ge(in_ffn, 8 * 16)
                    nc.vector.tensor_scalar(wup[:, 0:FH], wup[:, 0:FH], gam[:, 1:2], D ** 0.5, ALU.mult, ALU.mult).then_inc(wup_scaled, 1)
                    nc.vector.tensor_scalar(wup[:, FH:FH + FL], wup[:, FH:FH + FL], gam[:, 0:1], D ** 0.5, ALU.mult, ALU.mult).then_inc(wup_scaled, 1)

            run_steps(dve, step)

            def norm3(g):
                t3v = t3[:].rearrange("p (b d) -> p b d", b=GB)
                dve.wait_ge(x2b_ready, GB * (g + 1))
                dve.wait_ge(mm_y, g + 1)
                if g:
                    dve.wait_ge(out_ready, g)
                nc.vector.tensor_tensor(t3[:], bank(Y_BANK), x2b[:, g * (GB * D):(g + 1) * (GB * D)], ALU.add).then_inc(y_read, 1)
                dve.wait_ge(y_read, g + 1)
                for bb in range(GB):
                    last = nc.vector.bn_stats(st3[:, 6 * bb:6 * bb + 6], t3v[:, bb, :])
                last.then_inc(stats3_ready, 1)
                dve.wait_ge(stats3_ready, g + 1)
                for bb in range(GB):
                    last = nc.vector.bn_aggr(mv3[:, 2 * bb:2 * bb + 2], st3[:, 6 * bb:6 * bb + 6])
                last.then_inc(mv3_ready, 1)
                dve.wait_ge(rs3_ready, g + 1)
                for bb in range(GB):
                    col = (g * GB + bb) * D
                    last = nc.vector.tensor_scalar(x2b[:, col:col + D], t3v[:, bb, :], mv3[:, 2 * bb:2 * bb + 1],
                                                   rs3[:, bb:bb + 1], ALU.subtract, ALU.mult)
                last.then_inc(out_ready, 1)

            max2(LAST)
            sums2(LAST)
            block_diagonal(LAST, 0)
            block_diagonal(LAST, 1)
            norm3(0)
            regrouped(LAST)
            stats2(LAST, LAST % 2)
            x2_out(LAST)
            norm3(1)
            norm3(2)
            norm3(3)

        @block.tensor
        def _(pe):
            def product3(out_cols, w_hi_cols, w_lo_cols, m_hi, m_lo):
                nc.tensor.matmul(out_cols, w_hi_cols, m_hi, start=True, stop=False)
                nc.tensor.matmul(out_cols, w_hi_cols, m_lo, start=False, stop=False)
                return nc.tensor.matmul(out_cols, w_lo_cols, m_hi, start=False, stop=True)

            def project_qk(group, blk, before):
                for r in range(4):
                    u = 4 * "ABCD".index(blk) + r
                    before(r)
                    cols = slice(u * 128, (u + 1) * 128)
                    product3(bank(BLOCK_BANKS[blk][r]), wqk_hi[:, cols], wqk_lo[:, cols], xg_hi[:], xg_lo[:]).then_inc(mm_qk, 1)

            def project_k2(group, blk, before):
                for r in range(4):
                    c = 4 * "EF".index(blk) + r
                    before(r)
                    cols = slice(c * 128, (c + 1) * 128)
                    product3(bank(BLOCK_BANKS[blk][r]), wk2_hi[:, cols], wk2_lo[:, cols], cg_hi[:], cg_lo[:]).then_inc(mm_k2, 1)

            def transpose_p2(s):
                pe.wait_ge(p2_ready, s - 1)
                for ih in range(IH):
                    last = nc.tensor.transpose(bank(PT2)[:, ih * 128:(ih + 1) * 128], s2[:, ih * 128:(ih + 1) * 128], ident[:])
                last.then_inc(mm_pt2, 1)

            def weighted_v2(s, ih):
                pe.wait_ge(pb_ready, 2 * (s - 2) + ih + 1)
                for q in range(2 * J):
                    pp = q % 2
                    last = nc.tensor.matmul(bank(PV2[ih])[64 * pp:64 * pp + 64, (q // 2) * 128:(q // 2 + 1) * 128],
                                            v2[:, (q * IH + ih) * DH:(q * IH + ih + 1) * DH],
                                            pb[:, (ih * 2 * J + q) * 128:(ih * 2 * J + q + 1) * 128], start=True, stop=True)
                last.then_inc(mm_pv2, 1)

            def project_o2(s):
                pe.wait_ge(ot2_by_act, s - 1)
                pe.wait_ge(ot2_by_dve, s - 1)
                for k in range(K):
                    last = nc.tensor.matmul(bank(O2, D), ot2[:, k * 128:(k + 1) * 128], wo2[:, k * D:(k + 1) * D],
                                            start=k == 0, stop=k == K - 1)
                last.then_inc(mm_o2, 1)

            def transpose_x2(s, where):
                pe.wait_ge(xn_ready, s - 1)
                nc.tensor.transpose(bank(where, T), xn[:], ident[:]).then_inc(mm_x2t, 1)

            def step(s, h, g, phase, a, bc, d):
                par, b_par = phase % 2, 1 - phase % 2
                static = isinstance(s, int)

                late = not static or s > 2

                def read(r, before):
                    group, blk = before
                    if r < 2:
                        pe.wait_ge(qk_by_dve, dve_count(group, blk, r))
                    else:
                        pe.wait_ge(qk_by_act, act_count(group, blk, r))

                def read_k2(r, blk):
                    if r < 2:
                        pe.wait_ge(k2_by_dve, k2_dve_count(g, blk, r))
                    else:
                        pe.wait_ge(k2_by_act, k2_act_count(g, blk, r))

                def ring_wait(r):
                    if phase == 0 and a:
                        read(r, (g, "D"))
                    elif phase == 1 and a:
                        read_k2(r, "F")
                    elif r == 1 and late:
                        pe.wait_ge(sum2x_ready, s - 2)
                    elif r == 2:
                        pe.wait_ge(s2_ready, s - 1)

                def transpose_p(u):
                    if u % 2 == 0:
                        pe.wait_ge(p_ready, 2 * s - 2 + u // 2 + 1)
                    for i in range(4):
                        hd = 4 * u + i
                        last = nc.tensor.transpose(bank(T_BANK[u])[:, i * T:(i + 1) * T], p[:, hd * T:(hd + 1) * T], ident[:])
                    last.then_inc(mm_t, 1)

                if static and s == 0:
                    pe.wait_ge(x_lo, 1)
                    pe.wait_ge(w_lo, WQK_SPLIT[0])
                    project_qk(0, "A", lambda r: None)
                    pe.wait_ge(w_lo, WQK_SPLIT[1])
                    project_qk(0, "B", lambda r: read((r + 3) % 4, (0, "A")))
                    pe.wait_ge(w_lo, WQK_SPLIT[2])
                if static and s == 1:
                    pe.wait_ge(in_ident, 16)
                if bc:
                    transpose_p(0)
                    transpose_p(1)
                if phase == 0 and a:
                    project_qk(g, "C", lambda r: read(r, (g, "B")))
                    if static and s == 0:
                        pe.wait_ge(w_lo, WQK_SPLIT[3])
                if bc:
                    transpose_p(2)
                    transpose_p(3)
                if phase == 0 and a:
                    project_qk(g, "D", lambda r: read(r, (g, "C")))
                if phase == 1 and a:
                    project_k2(g, "F", lambda r: read_k2(r, "E"))
                if a:
                    if static and s == 0:
                        pe.wait_ge(w_lo, WV_SPLIT)
                    if bc:
                        pe.wait_ge(pt_ready, 4 * s - 4 + 2)
                    own = slice(phase * T, (phase + 1) * T)
                    for u in range(2):
                        cols = slice(u * BANK, (u + 1) * BANK)
                        nc.tensor.matmul(bank(V_BANK[u]), xg_lo[:, own], wv_hi[:, cols], start=True, stop=False)
                        nc.tensor.matmul(bank(V_BANK[u]), xg_hi[:, own], wv_hi[:, cols], start=False, stop=False)
                        nc.tensor.matmul(bank(V_BANK[u]), xg_hi[:, own], wv_lo[:, cols], start=False, stop=True).then_inc(mm_v, 1)
                if bc:
                    for u in range(2):
                        pe.wait_ge(pt_ready, 4 * s - 4 + u + 3)
                        if u == 0:
                            pe.wait_ge(v_ready, 2 * s)
                        for i in range(8):
                            hd = 8 * u + i
                            last = nc.tensor.matmul(bank(PV_BANK[u])[64 * (i % 2):64 * (i % 2) + 64, (i // 2) * T:(i // 2 + 1) * T],
                                                    v[b_par][:, hd * DH:(hd + 1) * DH], pt[:, hd * T:(hd + 1) * T], start=True, stop=True)
                        last.then_inc(mm_pv, 1)
                if bc:
                    if static and s == 1:
                        pe.wait_ge(w_lo, WV2_SPLIT)
                    own = slice((phase - 1) % GB * T, ((phase - 1) % GB + 1) * T)
                    for u in range(2):
                        ring_wait(u)
                        cols = slice(u * BANK, (u + 1) * BANK)
                        nc.tensor.matmul(bank(V2[u]), cg_lo[:, own], wv2_hi[:, cols], start=True, stop=False)
                        nc.tensor.matmul(bank(V2[u]), cg_hi[:, own], wv2_hi[:, cols], start=False, stop=False)
                        nc.tensor.matmul(bank(V2[u]), cg_hi[:, own], wv2_lo[:, cols], start=False, stop=True).then_inc(mm_v2, 1)
                    if static and s == 1:
                        pe.wait_ge(in_wo, 16)
                    if late:
                        if a:
                            pe.wait_ge(v_ready, 2 * s + 1)
                        transpose_x2(s - 1, V_BANK[0])
                    ring_wait(2)
                    pe.wait_ge(ot_ready, 2 * s)
                    for c in range(NC):
                        last = nc.tensor.matmul(bank(O, D), ot[:, c * T:(c + 1) * T], wo[:, c * D:(c + 1) * D],
                                                start=c == 0, stop=c == NC - 1)
                    last.then_inc(mm_o, 1)
                if d:
                    ring_wait(3)
                    transpose_p2(s)
                if a and phase == 0:
                    read(1, (g, "D"))
                    read(3, (g, "D"))
                if a:
                    pe.wait_ge(v_ready, 2 * s + 2)
                    if late:
                        pe.wait_ge(xnt_ready, s - 2)
                    for half in range(2):
                        for i in range(8):
                            hd = 8 * half + i
                            rows = slice(64 * (i % 2), 64 * (i % 2) + 64)
                            cols = slice(((hd // 2) * GB + phase) * T, ((hd // 2) * GB + phase + 1) * T)
                            mm = nc.tensor.matmul(bank(S_BANK[2 * half + i % 2])[:, (i // 2) * T:(i // 2 + 1) * T],
                                                  qt[rows, cols], kt[rows, cols], start=True, stop=True)
                            if i >= 6:
                                mm.then_inc(mm_s, 1)
                if bc:
                    if static and s == 1:
                        pe.wait_ge(in_perm, 16)
                    pe.wait_ge(v2s_ready, 2 * s - 2 + 1)
                    pe.wait_ge(x1_ready, s)
                    nc.tensor.transpose(bank(X1T, T), x1[:], perm[:]).then_inc(mm_x1t, 1)

                def project_q2(u):
                    for c in range(4):
                        last = nc.tensor.matmul(bank(Q2[u])[:, c * T:(c + 1) * T],
                                                wq2[:, (4 * u + c) * 128:(4 * u + c + 1) * 128], x1t[:], start=True, stop=True)
                    last.then_inc(mm_q2, 1)

                if d:
                    pe.wait_ge(v2_moved, 16 * 16 * (s - 1))
                    pe.wait_ge(v2s_ready, 2 * s)
                    weighted_v2(s, 0)
                if bc:
                    if static and s == 1:
                        pe.wait_ge(in_wq2, 16)
                    if d:
                        pe.wait_ge(pb_ready, 2 * (s - 2) + 2)
                    pe.wait_ge(x1t_ready, s)
                    project_q2(0)
                if d:
                    pe.wait_ge(sum1_ready, s)
                    weighted_v2(s, 1)
                if bc:
                    project_q2(1)
                if phase == 3 and not static:
                    pe.wait_ge(x_lo, g + 2)
                    after = [(ot2_by_act, s - 1), (ot2_by_dve, s - 1), (q2_ready, 2 * s - 1), (q2_ready, 2 * s)]
                    project_qk(g + 1, "A", lambda r: pe.wait_ge(*after[r]))
                    read(0, (g + 1, "A"))
                if d:
                    pe.wait_ge(in_wo2, 16)
                    project_o2(s)
                if phase == 3 and not static:
                    read(1, (g + 1, "A"))
                    read(2, (g + 1, "A"))
                if bc:
                    pe.wait_ge(sum1_ready, s)
                    pe.wait_ge(q2_ready, 2 * s)
                    if phase == 1:
                        read_k2(1, "F")
                        read_k2(3, "F")
                    for i in range(IH * K):
                        last = nc.tensor.matmul(bank(S2, BANK, 2)[:, i * H * J:(i + 1) * H * J],
                                                qb[:, i * 128:(i + 1) * 128],
                                                kt2[:].rearrange("p (b g t) -> p b g t", b=GB, g=H)[:, (phase - 1) % GB, :, J * i:J * i + J], start=True, stop=True)
                    last.then_inc(mm_s2, 1)
                if phase == 3 and not static:
                    def before_b(r):
                        if r == 0:
                            read(3, (g + 1, "A"))
                        elif r == 1:
                            pe.wait_ge(sum2x_ready, s - 1)
                        else:
                            pe.wait_ge(s2_ready, s)

                    project_qk(g + 1, "B", before_b)
                if phase == 0 and a:
                    if static and s == 0:
                        pe.wait_ge(w_lo, WK2_SPLIT)
                    pe.wait_ge(c_lo, g + 1)

                    def before_e(r):
                        if static and s == 0:
                            read(r, (0, "D"))
                        elif r == 1:
                            pe.wait_ge(sum2x_ready, s - 1)
                        elif r >= 2:
                            pe.wait_ge(s2_ready, s)

                    project_k2(g, "E", before_e)

            run_steps(pe, step)

            def up(g, c):
                m = 128 if c < NF - 1 else FL
                nc.tensor.matmul(bank(H_BANK[(NF * g + c) % 2])[0:m, :], wup[:, c * 128:c * 128 + m],
                                 xnt[:, g * (GB * T):(g + 1) * (GB * T)], start=True, stop=True).then_inc(mm_h, 1)

            def down(g, c):
                m = 128 if c < NF - 1 else FL
                pe.wait_ge(ht_ready, NF * g + c + 1)
                if c == 0 and g:
                    pe.wait_ge(y_read, g)
                for bb in range(GB):
                    w = wdn[:, c * D:(c + 1) * D] if c < NF - 1 else wdl[:]
                    last = nc.tensor.matmul(bank(Y_BANK)[:, bb * D:(bb + 1) * D], ht[c][0:m, bb * T:(bb + 1) * T], w,
                                            start=c == 0 and bb == 0, stop=c == NF - 1, skip_group_check=True)
                return last

            pe.wait_ge(wup_scaled, 2)
            for g in range(B // GB):
                pe.wait_ge(xnt_ready, GB * (g + 1))
                up(g, 0)
                up(g, 1)
                for c in range(NF):
                    if (g, c) == (0, 2):
                        transpose_p2(LAST)
                        transpose_x2(LAST - 1, X2T_BANK)
                    if (g, c) == (1, 0):
                        pe.wait_ge(v2_moved, 16 * 16 * B)
                        weighted_v2(LAST, 0)
                        weighted_v2(LAST, 1)
                    if (g, c) == (1, 4):
                        project_o2(LAST)
                    if (g, c) == (2, 3):
                        pe.wait_ge(xnt_ready, B - 1)
                        transpose_x2(LAST, X2T_BANK)
                    last = down(g, c)
                    if c + 2 < NF:
                        up(g, c + 2)
                last.then_inc(mm_y, 1)


def kernel(x, ctx_1024, L0_attn_W_Q, L0_attn_b_Q, L0_attn_W_K, L0_attn_b_K, L0_attn_W_V, L0_attn_b_V, L0_attn_W_O,
           L0_attn_b_O, L0_xattn_Wq, L0_xattn_bq, L0_xattn_Wk, L0_xattn_bk, L0_xattn_Wv, L0_xattn_bv, L0_xattn_Wo,
           L0_xattn_bo, L0_ffn_routing_token, L0_ffn_light_gamma, L0_ffn_light_w1, L0_ffn_light_b1, L0_ffn_light_w2,
           L0_ffn_light_b2, L0_ffn_heavy_gamma, L0_ffn_heavy_w1, L0_ffn_heavy_b1, L0_ffn_heavy_w2, L0_ffn_heavy_b2):
    import numpy as np
    import concourse.bacc as bacc
    from concourse.bass_utils import run_bass_kernel_spmd

    def a(z):
        return np.ascontiguousarray(np.asarray(z))

    def chunks(z):
        return a(np.asarray(z).reshape(-1, 128).T)

    order = np.arange(T).reshape(IH, J, 2, K).transpose(2, 0, 3, 1).reshape(-1)
    perm = np.zeros((T, T), np.float32)
    perm[order, np.arange(T)] = 1.0
    mask = np.zeros((128, K), np.float32)
    mask[np.arange(128), np.arange(128) // H] = 1.0
    x = np.asarray(x)
    c = np.asarray(ctx_1024)
    b_up = np.zeros((128, NF), np.float32)
    b_up[:, 0:NF - 1] = np.asarray(L0_ffn_heavy_b1).reshape(NF - 1, 128).T
    b_up[0:FL, NF - 1] = np.asarray(L0_ffn_light_b1)
    arrays = {
        "x_nat": a(x),
        "x_t": a(x.reshape(NG, GB, T, D).transpose(0, 3, 1, 2).reshape(NG, D, GB * T)),
        "ctx_t": a(c[:, order, :].reshape(NG, GB, T, D).transpose(0, 3, 1, 2).reshape(NG, D, GB * T)),
        "w_qk": a(np.concatenate([np.asarray(L0_attn_W_Q).reshape(HD, D).T, np.asarray(L0_attn_W_K).reshape(HD, D).T], 1)),
        "w_v": a(np.asarray(L0_attn_W_V).reshape(HD, D).T),
        "w_o": a(np.asarray(L0_attn_W_O).transpose(0, 2, 1).reshape(NC, 128, D).transpose(1, 0, 2).reshape(128, NC * D)),
        "b_qk": a(np.concatenate([chunks(np.asarray(L0_attn_b_Q).reshape(-1)), chunks(np.asarray(L0_attn_b_K).reshape(-1))], 1)),
        "b_v": chunks(np.asarray(L0_attn_b_V).reshape(-1)),
        "b_o": a(L0_attn_b_O),
        "w2_q": a(np.asarray(L0_xattn_Wq).T),
        "w2_k": a(np.asarray(L0_xattn_Wk).T),
        "w2_v": a(np.asarray(L0_xattn_Wv).T),
        "w2_o": a(np.asarray(L0_xattn_Wo).reshape(D, 2, K, DH).transpose(1, 3, 2, 0).reshape(128, K * D)),
        "b2_q": chunks(L0_xattn_bq),
        "b2_k": chunks(L0_xattn_bk),
        "b2_v": a(L0_xattn_bv),
        "b2_o": a(L0_xattn_bo),
        "w_up": a(np.concatenate([np.asarray(L0_ffn_heavy_w1), np.asarray(L0_ffn_light_w1)], 1)),
        "g_light": a(np.asarray(L0_ffn_light_gamma).reshape(D, 1)),
        "g_heavy": a(np.asarray(L0_ffn_heavy_gamma).reshape(D, 1)),
        "w_down": a(np.asarray(L0_ffn_heavy_w2).reshape(NF - 1, 128, D).transpose(1, 0, 2).reshape(128, (NF - 1) * D)),
        "w_down_light": a(L0_ffn_light_w2),
        "b_up": b_up,
        "bd_light": a(L0_ffn_light_b2),
        "bd_heavy": a(L0_ffn_heavy_b2),
        "ident_in": np.eye(128, dtype=np.float32),
        "perm_in": perm,
        "mask_in": mask,
    }
    nc = bacc.Bacc("TRN2", target_bir_lowering=False, num_devices=1)
    args = {n: nc.dram_tensor(n, z.shape, mybir.dt.from_np(z.dtype), kind="ExternalInput").ap() for n, z in arrays.items()}
    out = nc.dram_tensor("out", (B, T, D), mybir.dt.float32, kind="ExternalOutput").ap()
    build(nc, out=out, **args)
    r = run_bass_kernel_spmd(nc, [arrays], core_ids=[0])
    return r.results[0]["out"]
```

```python
from contextlib import ExitStack

import concourse.bass as bass
from concourse import mybir

B, T, D = 16, 128, 128
H, DH = 16, 64
HD = H * DH
NC = HD // 128
HALF = T // 2
IH, J, K = 2, 4, 8
FH, FL = 512, 64
NF = FH // 128 + 1
GB = 4
BANK = 512
EPS = 1e-5
NG = B // GB
WARM_PRODUCTS = 12


def build(nc, x_nat, x_t, ctx_t, w_qk, w_v, w_o, b_qk, b_v, b_o,
          w2_q, w2_k, w2_v, w2_o, b2_q, b2_k, b2_v, b2_o,
          w_up, g_light, g_heavy, w_down, w_down_light, b_up, bd_light, bd_heavy,
          ident_in, perm_in, mask_in, own_j_in, out):
    fp32 = mybir.dt.float32
    fp32r = mybir.dt.float32r
    ALU = mybir.AluOpType
    ACT = mybir.ActivationFunctionType
    AX = mybir.AxisListType

    ctx = ExitStack()
    with ctx:
        def sb(name, shape, dtype=fp32):
            return ctx.enter_context(nc.sbuf_tensor(name, shape, dtype))

        def sem(name):
            return ctx.enter_context(nc.semaphore(name))

        wqk_hi, wqk_lo = (sb("wqk_" + part, [128, 2 * HD], fp32r) for part in ("hi", "lo"))
        wv_hi, wv_lo = (sb("wv_" + part, [128, HD], fp32r) for part in ("hi", "lo"))
        wk2_hi, wk2_lo = (sb("wk2_" + part, [128, HD], fp32r) for part in ("hi", "lo"))
        wv2_hi, wv2_lo = (sb("wv2_" + part, [128, HD], fp32r) for part in ("hi", "lo"))
        wo = sb("wo", [128, NC * D])
        wq2 = sb("wq2", [128, HD])
        wo2 = sb("wo2", [128, K * D])
        wup_hi, wup_lo = (sb("wup_" + part, [128, FH + FL], fp32r) for part in ("hi", "lo"))
        wdn = sb("wdn", [128, (NF - 1) * D])
        wdl = sb("wdl", [FL, D])
        bqk = sb("bqk", [128, 2 * NC])
        bv = sb("bv", [128, NC])
        bo_row = sb("bo_row", [128, D])
        bq2 = sb("bq2", [128, NC])
        bk2 = sb("bk2", [128, NC])
        bv2_row = sb("bv2_row", [128, HD])
        bo2_row = sb("bo2_row", [128, D])
        bup = sb("bup", [128, NF])
        bdl_row = sb("bdl_row", [128, D])
        bdh_row = sb("bdh_row", [128, D])
        gam = sb("gam", [128, 2])
        ident = sb("ident", [128, 128])
        perm = sb("perm", [128, 128])
        mask = sb("mask", [128, K])
        own_j = sb("own_j", [128, J])
        minus_half = sb("minus_half", [128, 4])
        eps = sb("eps", [128, 4])
        warm = sb("warm", [128, 128])

        xg, xg_hi, xg_lo = sb("xg", [128, GB * T]), sb("xg_hi", [128, GB * T], fp32r), sb("xg_lo", [128, GB * T], fp32r)
        cg, cg_hi, cg_lo = sb("cg", [128, GB * T]), sb("cg_hi", [128, GB * T], fp32r), sb("cg_lo", [128, GB * T], fp32r)
        xres = [sb(f"xres{i}", [T, D]) for i in range(2)]
        qt = sb("qt", [128, NC * GB * T])
        kt = sb("kt", [128, NC * GB * T])
        v = [sb(f"v{i}", [T, HD]) for i in range(2)]
        p = sb("p", [T, H * T])
        neg_max = sb("neg_max", [T, H])
        row_sum = sb("row_sum", [T, H])
        row_inv = sb("row_inv", [T, H])
        pt = sb("pt", [T, H * T])
        ot = sb("ot", [128, NC * T])
        t1 = sb("t1", [T, D])
        st1 = sb("st1", [T, 6])
        mv1 = sb("mv1", [T, 2])
        ve1 = sb("ve1", [T, 1])
        rs1 = sb("rs1", [T, 1])
        x1 = sb("x1", [T, D])
        x1b = [sb(f"x1b{i}", [T, D]) for i in range(2)]
        x1t = sb("x1t", [128, T])
        qt2 = sb("qt2", [128, HALF * H])
        kb = sb("kb", [128, GB * HALF * 2 * H])
        v2s = sb("v2s", [T, HD])
        v2 = sb("v2", [128, J * 2 * IH * DH])
        s2 = sb("s2", [128, IH * K * H])
        p2 = sb("p2", [128, IH * K * H])
        mx2 = sb("mx2", [128, IH * K])
        sum2 = sb("sum2", [128, IH * K])
        inv2 = sb("inv2", [128, IH * K])
        pb = pt
        ot2 = ot
        t2 = sb("t2", [T, D])
        st2 = sb("st2", [T, 6])
        mv2 = sb("mv2", [T, 2])
        ve2 = sb("ve2", [T, 1])
        rs2 = sb("rs2", [T, 1])
        x2 = sb("x2", [T, D])
        sq = sb("sq", [T, D])
        ss = sb("ss", [T, 1])
        ssm = sb("ssm", [T, 1])
        rn = sb("rn", [T, 1])
        xn = sb("xn", [T, D])
        x2b = sb("x2b", [T, B * D])
        xnt = sb("xnt", [128, B * T])
        ht = [qt[:, c * GB * T:(c + 1) * GB * T] for c in range(NF)]
        t3 = kt[:, 0:GB * D]
        st3 = sb("st3", [T, GB * 6])
        mv3 = sb("mv3", [T, GB * 2])
        ve3 = sb("ve3", [T, GB])
        rs3 = sb("rs3", [T, GB])

        wqk, wv, wk2, wv2 = pt, p, ot, v2
        wup = x2b[:, (B - 5) * D:(B - 5) * D + FH + FL]
        fx_hi, fx_lo = [xg_hi, cg_hi], [xg_lo, cg_lo]

        ps = ctx.enter_context(nc.psum_tensor("ps", [128, 8 * BANK], fp32))

        def bank(n, cols=BANK, banks=1):
            return ps[:, n * BANK:n * BANK + (banks - 1) * BANK + cols]

        T_BANK = [7, 0, 1, 6]
        V_BANK = [7, 0]
        PV_BANK = [1, 6]
        S_BANK = [7, 0, 1, 6]
        V2, O, PT2, X1T, PV2, Q2, O2, S2 = [2, 3], 4, 5, 2, [3, 4], [5, 2], 3, 4
        BLOCK_BANKS = {"A": [3, 5, 4, 2], "B": [2, 3, 4, 5], "C": [2, 3, 4, 5], "D": [2, 3, 4, 5],
                       "E": [2, 3, 4, 5], "F": [2, 3, 4, 5]}
        FIRST_BANKS = S_BANK

        def dve_count(group, blk, r):
            return 8 * group + 2 * "ABCD".index(blk) + r + 1

        def act_count(group, blk, r):
            return 8 * group + 2 * "ABCD".index(blk) + r - 1

        def k2_dve_count(group, blk, r):
            return 4 * group + 2 * "EF".index(blk) + r + 1

        def k2_act_count(group, blk, r):
            return 4 * group + 2 * "EF".index(blk) + r - 1

        def k2_half(c, h2, ih, src):
            return (kb[64 * ih:64 * ih + 64, :].rearrange("p (b t e g) -> p b t e g", b=GB, e=2, g=H)[:, :, :, ih, 2 * c + h2],
                    src.rearrange("p (b e t) -> p b e t", b=GB, e=2)[64 * h2:64 * h2 + 64, :, ih, :])

        def ot2_half(ih):
            return (ot2[:].rearrange("p (k h e) -> p k h e", k=K, h=H)[:, :, :, ih * J:(ih + 1) * J].rearrange("p k h j -> p j k h"),
                    bank(PV2[ih]).rearrange("p (j k h) -> p j k h", j=J, k=K))

        H_BANK, Y_BANK, X2T_BANK = [0, 1], [7, 6], 2

        in_xres = [sem(f"in_xres{i}") for i in range(2)]
        in_xg, in_cg = sem("in_xg"), sem("in_cg")
        in_wqk = [sem(f"in_wqk{i}") for i in range(4)]
        in_bqk = sem("in_bqk")
        in_wv = sem("in_wv")
        in_ident = sem("in_ident")
        in_bv = sem("in_bv")
        in_wo = sem("in_wo")
        in_bo = sem("in_bo")
        in_perm = sem("in_perm")
        in_wk2 = sem("in_wk2")
        in_wq2 = sem("in_wq2")
        in_bqk2 = sem("in_bqk2")
        in_wv2 = sem("in_wv2")
        in_bv2 = sem("in_bv2")
        in_mask, in_own_j = sem("in_mask"), sem("in_own_j")
        in_wo2 = sem("in_wo2")
        in_bo2 = sem("in_bo2")
        in_ffn = sem("in_ffn")
        v2_moved = sem("v2_moved")
        out_stored = sem("out_stored")
        x_hi, x_lo, c_hi, c_lo, w_hi, w_lo = (sem(n) for n in ("x_hi", "x_lo", "c_hi", "c_lo", "w_hi", "w_lo"))
        f_hi, f_lo = sem("f_hi"), sem("f_lo")
        mm_qk, mm_v, mm_s, mm_t, mm_pv, mm_o = (sem(n) for n in ("mm_qk", "mm_v", "mm_s", "mm_t", "mm_pv", "mm_o"))
        mm_x1t, mm_k2, mm_q2, mm_v2, mm_s2 = (sem(n) for n in ("mm_x1t", "mm_k2", "mm_q2", "mm_v2", "mm_s2"))
        mm_pt2, mm_pv2, mm_o2, mm_x2t = (sem(n) for n in ("mm_pt2", "mm_pv2", "mm_o2", "mm_x2t"))
        mm_h, mm_y = sem("mm_h"), sem("mm_y")
        qk_by_dve, qk_by_act = sem("qk_by_dve"), sem("qk_by_act")
        v_ready, max_ready, exp_ready = (sem(n) for n in ("v_ready", "max_ready", "exp_ready"))
        inv_ready, p_ready, pt_ready, ot_ready = (sem(n) for n in ("inv_ready", "p_ready", "pt_ready", "ot_ready"))
        xres_ready, sum1_ready, stats1_ready, mv1_ready = (sem(n) for n in ("xres_ready", "sum1_ready", "stats1_ready", "mv1_ready"))
        ve1_ready, rs1_ready, x1_ready, x1b_ready, x1t_ready = (sem(n) for n in ("ve1_ready", "rs1_ready", "x1_ready", "x1b_ready", "x1t_ready"))
        k2_by_dve, k2_by_act = sem("k2_by_dve"), sem("k2_by_act")
        q2_ready, v2s_ready, s2_ready = (sem(n) for n in ("q2_ready", "v2s_ready", "s2_ready"))
        mx2_ready, sub2_ready, exp2_ready, sum2_ready, inv2_ready, p2_ready = (
            sem(n) for n in ("mx2_ready", "sub2_ready", "exp2_ready", "sum2_ready", "inv2_ready", "p2_ready"))
        pb_ready, ot2_by_act, ot2_by_dve = sem("pb_ready"), sem("ot2_by_act"), sem("ot2_by_dve")
        sum2x_ready, stats2_ready, mv2_ready, ve2_ready, rs2_ready = (
            sem(n) for n in ("sum2x_ready", "stats2_ready", "mv2_ready", "ve2_ready", "rs2_ready"))
        x2_ready, ss_ready, ssm_ready, rn_ready, xn_ready, xnt_ready, x2b_ready = (
            sem(n) for n in ("x2_ready", "ss_ready", "ssm_ready", "rn_ready", "xn_ready", "xnt_ready", "x2b_ready"))
        own_picked, zeroed, half_set, warm_set = (sem(n) for n in ("own_picked", "zeroed", "half_set", "warm_set"))
        bq_scaled, wup_scaled, wup_split, bd_summed = (sem(n) for n in ("bq_scaled", "wup_scaled", "wup_split", "bd_summed"))
        ht_ready, y_read, stats3_ready, mv3_ready, ve3_ready, rs3_ready, out_ready = (
            sem(n) for n in ("ht_ready", "y_read", "stats3_ready", "mv3_ready", "ve3_ready", "rs3_ready", "out_ready"))

        block = ctx.enter_context(nc.Block())

        FIRST_LOOPED, LAST_LOOPED, LAST = 3, 14, B + 1

        def run_steps(eng, step):
            for s in range(FIRST_LOOPED):
                step(s, s // 2, s // GB, s % GB, s < B, 1 <= s <= B, s >= 2)
            with eng.Fori(0, (LAST_LOOPED + 1 - FIRST_LOOPED) // GB) as i:
                for n in range(FIRST_LOOPED, FIRST_LOOPED + GB):
                    step(GB * i + n, GB // 2 * i + n // 2, i + n // GB, n % GB, True, True, True)
            for s in range(LAST_LOOPED + 1, LAST):
                step(s, s // 2, s // GB, s % GB, s < B, 1 <= s <= B, s >= 2)

        SPLITS = ([(wqk, wqk_hi, wqk_lo, u, in_wqk[u]) for u in range(4)] + [(wv, wv_hi, wv_lo, u, in_wv) for u in range(2)] +
                  [(wk2, wk2_hi, wk2_lo, u, in_wk2) for u in range(2)] + [(wv2, wv2_hi, wv2_lo, u, in_wv2) for u in range(2)])
        WQK_SPLIT, WV_SPLIT, WK2_SPLIT, WV2_SPLIT = [1, 2, 3, 4], 6, 8, 10

        @block.sync
        def _(sp):
            sp.dma_start(xg[:], x_t[0]).then_inc(in_xg, 16)
            for u in range(4):
                sp.dma_start(wqk[:, u * BANK:(u + 1) * BANK], w_qk[:, u * BANK:(u + 1) * BANK]).then_inc(in_wqk[u], 16)
            sp.dma_start(wv[:, 0:HD], w_v).then_inc(in_wv, 16)
            sp.dma_start(cg[:], ctx_t[0]).then_inc(in_cg, 16)
            for tile, src, s_in in ((wk2[:], w2_k, in_wk2), (wv2[:], w2_v, in_wv2), (bk2[:], b2_k, in_bqk2),
                                    (bq2[:], b2_q, in_bqk2), (ident[:], ident_in, in_ident), (bv[:], b_v, in_bv),
                                    (wo[:], w_o, in_wo), (perm[:], perm_in, in_perm), (wq2[:], w2_q, in_wq2),
                                    (xres[1][:], x_nat[1], in_xres[1]), (own_j[:], own_j_in, in_own_j),
                                    (mask[:], mask_in, in_mask), (wo2[:], w2_o, in_wo2)):
                sp.dma_start(tile, src).then_inc(s_in, 16)

            def step(s, h, g, phase, a, bc, d):
                b_par = 1 - phase % 2
                if phase == 3 and not isinstance(s, int):
                    sp.wait_ge(x_lo, g + 1)
                    sp.dma_start(xg[:], x_t[bass.ds(g + 1, 1)].rearrange("g p t -> p (g t)")).then_inc(in_xg, 16)
                    sp.wait_ge(c_lo, g + 1)
                    sp.dma_start(cg[:], ctx_t[bass.ds(g + 1, 1)].rearrange("g p t -> p (g t)")).then_inc(in_cg, 16)
                if a and bc and not (isinstance(s, int) and s == B - 1):
                    sp.wait_ge(sum1_ready, s)
                    sp.dma_start(xres[b_par][:], x_nat[bass.ds(s + 1, 1)].rearrange("b p t -> p (b t)")).then_inc(in_xres[b_par], 16)
                if bc:
                    if d:
                        sp.wait_ge(mm_pv2, 2 * s - 2)
                    else:
                        sp.wait_ge(v2s_ready, 2 * s)
                    for pp in range(2):
                        for j in range(J):
                            for ih in range(IH):
                                first = (ih * K * 2 + pp) * J + j
                                col = ((pp * J + j) * IH + ih) * DH
                                sp.dma_start(v2[:, col:col + DH],
                                             v2s[first:first + (K - 1) * 2 * J + 1:2 * J, :].rearrange("k (g d) -> k g d", g=H)
                                             ).then_inc(v2_moved, 16)

            run_steps(sp, step)
            with sp.Fori(0, B // GB) as g:
                sp.wait_ge(out_ready, g + 1)
                sp.dma_start(out[bass.ds(g * GB, GB)].rearrange("b t d -> t b d"),
                             x2b[:, bass.ds(g * (GB * D), GB * D)].rearrange("t (b d) -> t b d", b=GB)
                             ).then_inc(out_stored, 16)
            sp.wait_ge(out_stored, 16 * (B // GB))

        @block.gpsimd
        def _(pool):
            nc.gpsimd.memset(minus_half[:], -0.5).then_inc(half_set, 1)
            nc.gpsimd.memset(eps[:], EPS).then_inc(half_set, 1)
            nc.gpsimd.memset(kb[:], 0.0).then_inc(zeroed, 1)
            pool.dma_start(bo_row[:], b_o.partition_broadcast(128)).then_inc(in_bo, 16)
            pool.dma_start(bo2_row[:], b2_o.partition_broadcast(128)).then_inc(in_bo2, 16)
            pool.dma_start(bv2_row[:], b2_v.partition_broadcast(128)).then_inc(in_bv2, 16)
            for tile, src in ((bdl_row[:], bd_light.partition_broadcast(128)), (bdh_row[:], bd_heavy.partition_broadcast(128)),
                              (gam[:, 0:1], g_light), (gam[:, 1:2], g_heavy), (wup, w_up),
                              (wdn[:], w_down), (wdl[:], w_down_light), (bup[:], b_up)):
                pool.dma_start(tile, src).then_inc(in_ffn, 16)
            pool.wait_ge(in_bo, 16)
            pool.wait_ge(in_ffn, 8 * 16)
            nc.gpsimd.tensor_tensor(bdl_row[:], bdl_row[:], bdh_row[:], ALU.add).then_inc(bd_summed, 1)
            pool.wait_ge(bd_summed, 1)
            pool.wait_ge(half_set, 2)
            pool.wait_ge(in_bo2, 16)
            s2v = s2[:].rearrange("p (i g) -> p i g", g=H)

            def minus_max2(s):
                pool.wait_ge(mx2_ready, s - 1)
                nc.gpsimd.tensor_tensor(s2v, s2v, mx2[:].unsqueeze(2).to_broadcast([128, IH * K, H]),
                                        ALU.subtract).then_inc(sub2_ready, 1)

            def over_sum2(s):
                pool.wait_ge(inv2_ready, s - 1)
                nc.gpsimd.tensor_tensor(p2[:].rearrange("p (e k g) -> p k e g", e=IH, k=K),
                                        s2[:].rearrange("p (k e g) -> p k e g", k=K, e=IH),
                                        inv2[:].rearrange("p (k e) -> p k e", k=K).unsqueeze(3).to_broadcast([128, K, IH, H]),
                                        ALU.mult).then_inc(p2_ready, 1)

            def rstd2(s):
                pool.wait_ge(mv2_ready, s - 1)
                nc.gpsimd.tensor_tensor(ve2[:], mv2[:, 1:2], eps[:, 0:1], ALU.add).then_inc(ve2_ready, 1)
                pool.wait_ge(ve2_ready, s - 1)
                nc.gpsimd.tensor_tensor(rs2[:], ve2[:], minus_half[:, 0:1], ALU.pow).then_inc(rs2_ready, 1)

            def rms2(s):
                pool.wait_ge(ssm_ready, s - 1)
                nc.gpsimd.tensor_tensor(rn[:], ssm[:], minus_half[:, 0:1], ALU.pow).then_inc(rn_ready, 1)
                nc.gpsimd.tensor_tensor(x2b[:, bass.ds((s - 2) * D, D)], x2[:], bdl_row[:], ALU.add).then_inc(x2b_ready, 1)

            def step(s, h, g, phase, a, bc, d):
                par, b_par = phase % 2, 1 - phase % 2
                if a:
                    pool.wait_ge(in_xres[par], 16 * (h + 1))
                    nc.gpsimd.tensor_tensor(xres[par][:], xres[par][:], bo_row[:], ALU.add).then_inc(xres_ready, 1)
                if d:
                    over_sum2(s)
                if bc:
                    pool.wait_ge(mv1_ready, s)
                    nc.gpsimd.tensor_tensor(ve1[:], mv1[:, 1:2], eps[:, 0:1], ALU.add).then_inc(ve1_ready, 1)
                    pool.wait_ge(ve1_ready, s)
                    nc.gpsimd.tensor_tensor(rs1[:], ve1[:], minus_half[:, 0:1], ALU.pow).then_inc(rs1_ready, 1)
                    pool.wait_ge(x1_ready, s)
                    nc.gpsimd.tensor_tensor(x1b[b_par][:], x1[:], bo2_row[:], ALU.add).then_inc(x1b_ready, 1)
                for half in range(2):
                    if a:
                        pool.wait_ge(inv_ready, 2 * s + half + 1)
                        ph = p[:, half * 8 * T:(half + 1) * 8 * T].rearrange("q (h k) -> q h k", h=8)
                        nc.gpsimd.tensor_tensor(ph, ph, row_inv[:, 8 * half:8 * half + 8].unsqueeze(2).to_broadcast([T, 8, T]),
                                                ALU.mult).then_inc(p_ready, 1)
                if d:
                    rstd2(s)
                if bc:
                    minus_max2(s + 1)
                if d:
                    rms2(s)

            run_steps(pool, step)
            for g in range(B // GB):
                if g == 1:
                    over_sum2(LAST)
                    rstd2(LAST)
                    rms2(LAST)
                pool.wait_ge(mv3_ready, g + 1)
                nc.gpsimd.tensor_tensor(ve3[:], mv3[:].rearrange("p (b m) -> p b m", m=2)[:, :, 1], eps[:], ALU.add).then_inc(ve3_ready, 1)
                pool.wait_ge(ve3_ready, g + 1)
                nc.gpsimd.tensor_tensor(rs3[:], ve3[:], minus_half[:], ALU.pow).then_inc(rs3_ready, 1)

        @block.scalar
        def _(act):
            act.dma_start(bqk[:], b_qk).then_inc(in_bqk, 16)
            act.dma_start(xres[0][:], x_nat[0]).then_inc(in_xres[0], 16)

            def split_hi(n):
                tile, hi, _, u, loaded = SPLITS[n]
                act.wait_ge(loaded, 16)
                nc.scalar.activation(hi[:, u * BANK:(u + 1) * BANK], tile[:, u * BANK:(u + 1) * BANK], ACT.Copy).then_inc(w_hi, 1)

            def x_high(group):
                act.wait_ge(in_xg, 16 * group + 16)
                nc.scalar.activation(xg_hi[:], xg[:], ACT.Copy).then_inc(x_hi, 1)

            def c_high(group):
                act.wait_ge(in_cg, 16 * group + 16)
                nc.scalar.activation(cg_hi[:], cg[:], ACT.Copy).then_inc(c_hi, 1)

            def qk_out(group, blk, banks=None):
                banks = banks or BLOCK_BANKS[blk]
                for r in (2, 3):
                    u = 4 * "ABCD".index(blk) + r
                    dst = (qt if u < NC else kt)[:, (u % NC) * GB * T:(u % NC + 1) * GB * T]
                    act.wait_ge(mm_qk, 16 * group + u + 1)
                    nc.scalar.activation(dst, bank(banks[r]), ACT.Identity, bias=bqk[:, u:u + 1],
                                         scale=DH ** -0.5 if u < NC else 1.0).then_inc(qk_by_act, 1)

            def k2_out(group, blk):
                for r in (2, 3):
                    c = 4 * "EF".index(blk) + r
                    act.wait_ge(mm_k2, 8 * group + c + 1)
                    for h2 in range(2):
                        for ih in range(IH):
                            dst, src = k2_half(c, h2, ih, bank(BLOCK_BANKS[blk][r]))
                            last = nc.scalar.activation(dst, src, ACT.Identity, bias=bk2[64 * h2:64 * h2 + 64, c:c + 1])
                    last.then_inc(k2_by_act, 1)

            def exp2(s):
                act.wait_ge(sub2_ready, s - 1)
                nc.scalar.activation(s2[:], s2[:], ACT.Exp, scale=DH ** -0.5).then_inc(exp2_ready, 1)

            def regrouped(s):
                act.wait_ge(mm_pv2, 2 * (s - 2) + 1)
                dst, src = ot2_half(0)
                nc.scalar.activation(dst, src, ACT.Copy).then_inc(ot2_by_act, 1)

            def normed_x2(s):
                act.wait_ge(rn_ready, s - 1)
                nc.scalar.activation(xn[:], x2[:], ACT.Copy, scale=rn[:, 0:1]).then_inc(xn_ready, 1)

            def x2_transposed(s, where):
                act.wait_ge(mm_x2t, s - 1)
                nc.scalar.activation(xnt[:, bass.ds((s - 2) * T, T)], bank(where, T), ACT.Copy).then_inc(xnt_ready, 1)

            def f_high(g, batches=GB):
                act.wait_ge(xnt_ready, GB * g + batches)
                if g == 0:
                    act.wait_ge(mm_v, 2 * B)
                if g == 1:
                    act.wait_ge(mm_v2, 2 * B)
                if g > 1:
                    act.wait_ge(mm_h, NF * (g - 1))
                nc.scalar.activation(fx_hi[g % 2][:, 0:batches * T], xnt[:, g * GB * T:(g * GB + batches) * T], ACT.Copy).then_inc(f_hi, 1)

            def gelu(g, c):
                m = 128 if c < NF - 1 else FL
                act.wait_ge(mm_h, NF * g + c + 1)
                nc.scalar.activation(ht[c][0:m, :], bank(H_BANK[(NF * g + c) % 2])[0:m, :], ACT.Gelu,
                                     bias=bup[0:m, c:c + 1]).then_inc(ht_ready, 1)

            def step(s, h, g, phase, a, bc, d):
                par, b_par = phase % 2, 1 - phase % 2

                def transposed(u):
                    act.wait_ge(mm_t, 4 * s - 4 + u + 1)
                    nc.scalar.activation(pt[:, u * BANK:(u + 1) * BANK], bank(T_BANK[u]), ACT.Copy).then_inc(pt_ready, 1)

                def exponentials(q):
                    act.wait_ge(max_ready, 4 * s + q + 1)
                    for pos in range(4):
                        hd = 8 * (q // 2) + 2 * pos + q % 2
                        last = nc.scalar.activation(p[:, hd * T:(hd + 1) * T], bank(S_BANK[q])[:, pos * T:(pos + 1) * T], ACT.Exp,
                                                    bias=neg_max[:, hd:hd + 1], accum_out=row_sum[:, hd:hd + 1])
                    last.then_inc(exp_ready, 1)

                static = isinstance(s, int)
                if static and s == 0:
                    x_high(0)
                    split_hi(0)
                    split_hi(1)
                    split_hi(2)
                    act.wait_ge(bq_scaled, 1)
                    qk_out(0, "A", FIRST_BANKS)
                    split_hi(3)
                    qk_out(0, "B")
                if static and s == LAST - 1:
                    f_high(0)
                if bc:
                    transposed(0)
                    transposed(1)
                if phase == 0 and a and bc:
                    qk_out(g, "B")
                if phase == 1 and a:
                    if static:
                        act.wait_ge(in_bqk2, 32)
                        act.wait_ge(zeroed, 1)
                    k2_out(g, "E")
                if phase == 0 and a:
                    qk_out(g, "C")
                if static and s == 0:
                    split_hi(4)
                    split_hi(5)
                if bc:
                    transposed(2)
                    transposed(3)
                if d:
                    exp2(s)
                if phase == 0 and a:
                    qk_out(g, "D")
                if phase == 1 and a:
                    k2_out(g, "F")
                if a:
                    for u in range(2):
                        act.wait_ge(mm_v, 2 * s + u + 1)
                        nc.scalar.activation(v[par][:, u * BANK:(u + 1) * BANK], bank(V_BANK[u]), ACT.Copy).then_inc(v_ready, 1)
                if static and s == 0:
                    c_high(0)
                    for n in range(6, 10):
                        split_hi(n)
                if not static or s > 2:
                    normed_x2(s - 1)
                    x2_transposed(s - 1, V_BANK[0])
                if a:
                    exponentials(0)
                if phase == 0 and bc and a:
                    act.wait_ge(mm_v2, 2 * s)
                    c_high(g)
                if static and s == LAST - 1:
                    act.wait_ge(in_ffn, 8 * 16)
                    gelu(0, 0)
                    gelu(0, 1)
                if bc:
                    act.wait_ge(mm_x1t, s)
                    nc.scalar.activation(x1t[:], bank(X1T, T), ACT.Copy).then_inc(x1t_ready, 1)
                if a:
                    exponentials(1)
                if phase == 3 and not static:
                    act.wait_ge(mm_v, 2 * s + 2)
                    x_high(g + 1)
                if d:
                    regrouped(s)
                if static and s == LAST - 1:
                    for c in range(2, NF):
                        gelu(0, c)
                    f_high(1)
                if a:
                    exponentials(2)
                    exponentials(3)
                if phase == 3 and not static:
                    qk_out(g + 1, "A")

            run_steps(act, step)
            for g in range(1, NG):
                for c in range(NF):
                    if (g, c) == (1, 2):
                        exp2(LAST)
                        normed_x2(LAST - 1)
                    if (g, c) == (1, 4):
                        x2_transposed(LAST - 1, X2T_BANK)
                    if (g, c) == (1, 0):
                        f_high(2)
                    if (g, c) == (2, 0):
                        regrouped(LAST)
                    if (g, c) == (2, 1):
                        f_high(3, GB - 1)
                    gelu(g, c)
                if g == 2:
                    normed_x2(LAST)
                    act.wait_ge(mm_x2t, B)
                    nc.scalar.activation(fx_hi[1][:, (GB - 1) * T:GB * T], bank(X2T_BANK, T), ACT.Copy).then_inc(f_hi, 1)

        @block.vector
        def _(dve):
            nc.vector.memset(warm[:], 0.0).then_inc(warm_set, 1)
            dve.wait_ge(in_bqk, 16)
            nc.vector.tensor_scalar(bqk[:, 0:NC], bqk[:, 0:NC], DH ** -0.5, None, ALU.mult).then_inc(bq_scaled, 1)
            dve.wait_ge(bq_scaled, 1)
            s2v = s2[:].rearrange("p (i g) -> p i g", g=H)

            def split_lo(n):
                tile, hi, lo, u, _ = SPLITS[n]
                cols = slice(u * BANK, (u + 1) * BANK)
                dve.wait_ge(w_hi, n + 1)
                nc.vector.tensor_tensor(lo[:, cols], tile[:, cols], hi[:, cols].bitcast(fp32), ALU.subtract).then_inc(w_lo, 1)

            def x_low(group):
                dve.wait_ge(x_hi, group + 1)
                nc.vector.tensor_tensor(xg_lo[:], xg[:], xg_hi[:].bitcast(fp32), ALU.subtract).then_inc(x_lo, 1)

            def c_low(group):
                dve.wait_ge(c_hi, group + 1)
                nc.vector.tensor_tensor(cg_lo[:], cg[:], cg_hi[:].bitcast(fp32), ALU.subtract).then_inc(c_lo, 1)

            def qk_out(group, blk, banks=None):
                banks = banks or BLOCK_BANKS[blk]
                for r in (0, 1):
                    u = 4 * "ABCD".index(blk) + r
                    dst = (qt if u < NC else kt)[:, (u % NC) * GB * T:(u % NC + 1) * GB * T]
                    dve.wait_ge(mm_qk, 16 * group + u + 1)
                    nc.vector.tensor_scalar(dst, bank(banks[r]), DH ** -0.5 if u < NC else 1.0, bqk[:, u:u + 1],
                                            ALU.mult, ALU.add).then_inc(qk_by_dve, 1)

            def k2_out(group, blk):
                for r in (0, 1):
                    c = 4 * "EF".index(blk) + r
                    dve.wait_ge(mm_k2, 8 * group + c + 1)
                    for h2 in range(2):
                        for ih in range(IH):
                            dst, src = k2_half(c, h2, ih, bank(BLOCK_BANKS[blk][r]))
                            last = nc.vector.tensor_scalar(dst, src, bk2[64 * h2:64 * h2 + 64, c:c + 1], None, ALU.add)
                    last.then_inc(k2_by_dve, 1)

            def regrouped(s):
                dve.wait_ge(mm_pv2, 2 * (s - 2) + 2)
                dst, src = ot2_half(1)
                nc.vector.tensor_copy(dst, src).then_inc(ot2_by_dve, 1)

            def max2(s):
                dve.wait_ge(s2_ready, s - 1)
                nc.vector.reduce_max(mx2[:], s2v, AX.X).then_inc(mx2_ready, 1)

            def sums2(s):
                dve.wait_ge(exp2_ready, s - 1)
                nc.vector.reduce_sum(sum2[:], s2v, AX.X).then_inc(sum2_ready, 1)
                dve.wait_ge(sum2_ready, s - 1)
                nc.vector.reciprocal(inv2[:], sum2[:]).then_inc(inv2_ready, 1)

            def block_diagonal(s, ih):
                dve.wait_ge(mm_pt2, s - 1)
                o = pb[:, ih * 1024:(ih + 1) * 1024].rearrange("p (q k h) -> p q k h", q=2 * J, k=K)
                i = bank(PT2)[:, ih * 128:(ih + 1) * 128].rearrange("p (q h) -> p q h", h=H)
                nc.vector.tensor_tensor(o, i.unsqueeze(2).to_broadcast([128, 2 * J, K, H]),
                                        mask[:].unsqueeze(1).unsqueeze(3).to_broadcast([128, 2 * J, K, H]),
                                        ALU.mult).then_inc(pb_ready, 1)

            def stats2(s, par):
                dve.wait_ge(mm_o2, s - 1)
                dve.wait_ge(x1b_ready, s - 1)
                nc.vector.tensor_tensor(t2[:], bank(O2, D), x1b[par][:], ALU.add).then_inc(sum2x_ready, 1)
                dve.wait_ge(sum2x_ready, s - 1)
                nc.vector.bn_stats(st2[:], t2[:]).then_inc(stats2_ready, 1)
                dve.wait_ge(bq_scaled, 1)
                dve.wait_ge(stats2_ready, s - 1)
                nc.vector.bn_aggr(mv2[:], st2[:]).then_inc(mv2_ready, 1)

            def x2_out(s):
                if not (isinstance(s, int) and s == 2):
                    dve.wait_ge(x2b_ready, s - 2)
                    dve.wait_ge(xn_ready, s - 2)
                dve.wait_ge(rs2_ready, s - 1)
                nc.vector.tensor_scalar(x2[:], t2[:], mv2[:, 0:1], rs2[:, 0:1], ALU.subtract, ALU.mult).then_inc(x2_ready, 1)
                dve.wait_ge(x2_ready, s - 1)
                nc.vector.tensor_tensor_reduce(out=sq[:], in0=x2[:], in1=x2[:], scale=1.0, scalar=0.0,
                                               op0=ALU.mult, op1=ALU.add, accum_out=ss[:, 0:1]).then_inc(ss_ready, 1)
                dve.wait_ge(ss_ready, s - 1)
                nc.vector.tensor_scalar(ssm[:], ss[:], 1e-24, None, ALU.max).then_inc(ssm_ready, 1)

            def f_low(g, batches=GB):
                dve.wait_ge(f_hi, g + 1)
                nc.vector.tensor_tensor(fx_lo[g % 2][:, 0:batches * T], xnt[:, g * GB * T:(g * GB + batches) * T],
                                        fx_hi[g % 2][:, 0:batches * T].bitcast(fp32), ALU.subtract).then_inc(f_lo, 1)

            def step(s, h, g, phase, a, bc, d):
                par, b_par = phase % 2, 1 - phase % 2
                static = isinstance(s, int)

                def q2_out(u):
                    dve.wait_ge(mm_q2, 2 * s - 2 + u + 1)
                    src = bank(Q2[u]).rearrange("p (c e t) -> p c e t", c=4, e=2)
                    for h2 in range(2):
                        rows = slice(64 * h2, 64 * h2 + 64)
                        for ih in range(IH):
                            o = qt2[64 * ih:64 * ih + 64, :].rearrange("p (t h) -> p t h", h=H)[:, :, 8 * u + h2:8 * u + 8:2]
                            last = nc.vector.tensor_tensor(o, src[rows, :, ih, :].rearrange("p c t -> p t c"),
                                                           bq2[rows, 4 * u:4 * u + 4].unsqueeze(1).to_broadcast([64, HALF, 4]), ALU.add)
                    last.then_inc(q2_ready, 1)

                def score_max(q):
                    first = 8 * (q // 2) + q % 2
                    dve.wait_ge(mm_s, 4 * s + q + 1)
                    nc.vector.reduce_max(neg_max[:, first:first + 7:2], bank(S_BANK[q]).rearrange("p (h k) -> p h k", h=4),
                                         AX.X, negate=True).then_inc(max_ready, 1)

                if static and s == 0:
                    x_low(0)
                    split_lo(0)
                    split_lo(1)
                    split_lo(2)
                    qk_out(0, "A", FIRST_BANKS)
                    split_lo(3)
                    qk_out(0, "B")
                if static and s == LAST - 1:
                    f_low(0)
                if phase == 0 and a:
                    qk_out(g, "C")
                if static and s == 0:
                    split_lo(4)
                    split_lo(5)
                if d:
                    sums2(s)
                if phase == 0 and a:
                    qk_out(g, "D")
                if phase == 1 and a:
                    k2_out(g, "F")
                if static and s == 0:
                    c_low(0)
                if bc:
                    if static and s == 1:
                        dve.wait_ge(in_bv, 16)
                    for u in range(2):
                        dve.wait_ge(mm_pv, 2 * s - 2 + u + 1)
                        nc.vector.tensor_tensor(ot[:, u * BANK:(u + 1) * BANK].rearrange("p (c t) -> p c t", c=4),
                                                bank(PV_BANK[u]).rearrange("p (c t) -> p c t", c=4),
                                                bv[:, 4 * u:4 * u + 4].unsqueeze(2).to_broadcast([128, 4, T]),
                                                ALU.add).then_inc(ot_ready, 1)
                    if static and s == 1:
                        dve.wait_ge(in_bv2, 16)
                    if d:
                        dve.wait_ge(v2_moved, 16 * 16 * (s - 1))
                    for u in range(2):
                        dve.wait_ge(mm_v2, 2 * s - 2 + u + 1)
                        nc.vector.tensor_tensor(v2s[:, u * BANK:(u + 1) * BANK], bank(V2[u]),
                                                bv2_row[:, u * BANK:(u + 1) * BANK], ALU.add).then_inc(v2s_ready, 1)
                    dve.wait_ge(mm_o, s)
                    dve.wait_ge(xres_ready, s)
                    nc.vector.tensor_tensor(t1[:], bank(O, D), xres[b_par][:], ALU.add).then_inc(sum1_ready, 1)
                    dve.wait_ge(sum1_ready, s)
                    nc.vector.bn_stats(st1[:], t1[:]).then_inc(stats1_ready, 1)
                    dve.wait_ge(bq_scaled, 1)
                    dve.wait_ge(stats1_ready, s)
                    nc.vector.bn_aggr(mv1[:], st1[:]).then_inc(mv1_ready, 1)
                if d:
                    if static and s == 2:
                        dve.wait_ge(in_mask, 16)
                    block_diagonal(s, 0)
                if a:
                    score_max(0)
                if bc:
                    dve.wait_ge(rs1_ready, s)
                    nc.vector.tensor_scalar(x1[:], t1[:], mv1[:, 0:1], rs1[:, 0:1], ALU.subtract, ALU.mult).then_inc(x1_ready, 1)
                if a:
                    score_max(1)
                if d:
                    block_diagonal(s, 1)
                if a:
                    score_max(2)
                    score_max(3)
                if static and s == 0:
                    split_lo(6)
                    split_lo(7)
                if phase == 3 and not static:
                    x_low(g + 1)
                if bc:
                    if static and s == 1:
                        dve.wait_ge(in_own_j, 16)
                    q2_out(0)
                if d:
                    regrouped(s)
                if a:
                    dve.wait_ge(exp_ready, 4 * s + 2)
                    nc.vector.reciprocal(row_inv[:, 0:8], row_sum[:, 0:8]).then_inc(inv_ready, 1)
                if static and s == 0:
                    split_lo(8)
                    split_lo(9)
                if bc:
                    q2_out(1)
                if phase == 0 and a and bc:
                    c_low(g)
                if phase == 3 and not static:
                    qk_out(g + 1, "A")
                if a:
                    dve.wait_ge(exp_ready, 4 * s + 4)
                    nc.vector.reciprocal(row_inv[:, 8:16], row_sum[:, 8:16]).then_inc(inv_ready, 1)
                if d:
                    stats2(s, par)
                if static and s == LAST - 1:
                    f_low(1)
                if bc:
                    dve.wait_ge(mm_s2, s)
                    scores = bank(S2, BANK, 2).rearrange("p (k j n) -> p k j n", k=K, j=J)
                    own = s2[:].rearrange("p (k n) -> p k n", k=K)
                    nc.vector.tensor_scalar(own, scores[:, :, 0], own_j[:, 0:1], None, ALU.mult).then_inc(own_picked, 1)
                    for j in range(1, J):
                        dve.wait_ge(own_picked, (J - 1) * s - (J - 1) + j)
                        nc.vector.scalar_tensor_tensor(out=own, in0=scores[:, :, j], scalar=own_j[:, j:j + 1], in1=own,
                                                       op0=ALU.mult, op1=ALU.add).then_inc(own_picked if j < J - 1 else s2_ready, 1)
                    max2(s + 1)
                if static and s == 0:
                    dve.wait_ge(in_bqk2, 32)
                    dve.wait_ge(zeroed, 1)
                if phase == 0 and a:
                    k2_out(g, "E")
                if phase == 3 and not static:
                    qk_out(g + 1, "B")
                if d:
                    x2_out(s)
                if static and s == 1:
                    dve.wait_ge(in_ffn, 8 * 16)
                    nc.vector.tensor_scalar(wup[:, 0:FH], wup[:, 0:FH], gam[:, 1:2], D ** 0.5, ALU.mult, ALU.mult).then_inc(wup_scaled, 1)
                    nc.vector.tensor_scalar(wup[:, FH:FH + FL], wup[:, FH:FH + FL], gam[:, 0:1], D ** 0.5, ALU.mult, ALU.mult).then_inc(wup_scaled, 1)
                    dve.wait_ge(wup_scaled, 2)
                    nc.vector.tensor_copy(wup_hi[:], wup).then_inc(wup_split, 1)
                    dve.wait_ge(wup_split, 1)
                    nc.vector.tensor_tensor(wup_lo[:], wup, wup_hi[:].bitcast(fp32), ALU.subtract).then_inc(wup_split, 1)

            run_steps(dve, step)

            t3v = t3.rearrange("p (b d) -> p b d", b=GB)

            def y_out(g):
                dve.wait_ge(x2b_ready, GB * (g + 1))
                dve.wait_ge(mm_y, g + 1)
                if g:
                    dve.wait_ge(out_ready, g)
                nc.vector.tensor_tensor(t3, bank(Y_BANK[g % 2]), x2b[:, g * (GB * D):(g + 1) * (GB * D)], ALU.add).then_inc(y_read, 1)

            def norm3(g):
                dve.wait_ge(y_read, g + 1)
                for bb in range(GB):
                    last = nc.vector.bn_stats(st3[:, 6 * bb:6 * bb + 6], t3v[:, bb, :])
                last.then_inc(stats3_ready, 1)
                dve.wait_ge(stats3_ready, g + 1)
                for bb in range(GB):
                    last = nc.vector.bn_aggr(mv3[:, 2 * bb:2 * bb + 2], st3[:, 6 * bb:6 * bb + 6])
                last.then_inc(mv3_ready, 1)
                dve.wait_ge(rs3_ready, g + 1)
                for bb in range(GB):
                    col = (g * GB + bb) * D
                    last = nc.vector.tensor_scalar(x2b[:, col:col + D], t3v[:, bb, :], mv3[:, 2 * bb:2 * bb + 1],
                                                   rs3[:, bb:bb + 1], ALU.subtract, ALU.mult)
                last.then_inc(out_ready, 1)

            y_out(0)
            f_low(2)
            norm3(0)
            sums2(LAST)
            block_diagonal(LAST, 0)
            block_diagonal(LAST, 1)
            regrouped(LAST)
            y_out(1)
            f_low(3, GB - 1)
            stats2(LAST, LAST % 2)
            x2_out(LAST)
            last_cols = slice((GB - 1) * T, GB * T)
            dve.wait_ge(f_hi, NG + 1)
            nc.vector.tensor_tensor(fx_lo[1][:, last_cols], bank(X2T_BANK, T), fx_hi[1][:, last_cols].bitcast(fp32),
                                    ALU.subtract).then_inc(f_lo, 1)
            norm3(1)
            for g in range(2, NG):
                y_out(g)
                norm3(g)

        @block.tensor
        def _(pe):
            pe.wait_ge(warm_set, 1)
            for _ in range(WARM_PRODUCTS):
                nc.tensor.matmul(bank(O, D), warm[:], warm[:], start=True, stop=True)

            def product3(out_cols, w_hi_cols, w_lo_cols, m_hi, m_lo):
                nc.tensor.matmul(out_cols, w_hi_cols, m_hi, start=True, stop=False)
                nc.tensor.matmul(out_cols, w_hi_cols, m_lo, start=False, stop=False)
                return nc.tensor.matmul(out_cols, w_lo_cols, m_hi, start=False, stop=True)

            def project_qk(group, blk, before, banks=None, units=range(4)):
                for r in units:
                    u = 4 * "ABCD".index(blk) + r
                    before(r)
                    cols = slice(u * 128, (u + 1) * 128)
                    product3(bank((banks or BLOCK_BANKS[blk])[r]), wqk_hi[:, cols], wqk_lo[:, cols], xg_hi[:], xg_lo[:]).then_inc(mm_qk, 1)

            def project_k2(group, blk, before, units=range(4)):
                for r in units:
                    c = 4 * "EF".index(blk) + r
                    before(r)
                    cols = slice(c * 128, (c + 1) * 128)
                    product3(bank(BLOCK_BANKS[blk][r]), wk2_hi[:, cols], wk2_lo[:, cols], cg_hi[:], cg_lo[:]).then_inc(mm_k2, 1)

            def transpose_p2(s):
                pe.wait_ge(p2_ready, s - 1)
                for ih in range(IH):
                    last = nc.tensor.transpose(bank(PT2)[:, ih * 128:(ih + 1) * 128], p2[:, ih * 128:(ih + 1) * 128], ident[:])
                last.then_inc(mm_pt2, 1)

            def weighted_v2(s, ih):
                pe.wait_ge(pb_ready, 2 * (s - 2) + ih + 1)
                for n in range(2 * J):
                    j, pp = n // 2, n % 2
                    q = pp * J + j
                    last = nc.tensor.matmul(bank(PV2[ih])[64 * pp:64 * pp + 64, j * 128:(j + 1) * 128],
                                            v2[:, (q * IH + ih) * DH:(q * IH + ih + 1) * DH],
                                            pb[:, (ih * 2 * J + q) * 128:(ih * 2 * J + q + 1) * 128], start=True, stop=True)
                last.then_inc(mm_pv2, 1)

            def project_o2(s):
                pe.wait_ge(ot2_by_act, s - 1)
                pe.wait_ge(ot2_by_dve, s - 1)
                for k in range(K):
                    last = nc.tensor.matmul(bank(O2, D), ot2[:, k * 128:(k + 1) * 128], wo2[:, k * D:(k + 1) * D],
                                            start=k == 0, stop=k == K - 1)
                last.then_inc(mm_o2, 1)

            def transpose_x2(s, where):
                pe.wait_ge(xn_ready, s - 1)
                nc.tensor.transpose(bank(where, T), xn[:], ident[:]).then_inc(mm_x2t, 1)

            def up(g, c):
                m = 128 if c < NF - 1 else FL
                cols = slice(c * 128, c * 128 + m)
                product3(bank(H_BANK[(NF * g + c) % 2])[0:m, :], wup_hi[:, cols], wup_lo[:, cols],
                         fx_hi[g % 2][:], fx_lo[g % 2][:]).then_inc(mm_h, 1)

            def down(g, c):
                m = 128 if c < NF - 1 else FL
                pe.wait_ge(ht_ready, NF * g + c + 1)
                if c == 0 and g > 1:
                    pe.wait_ge(y_read, g - 1)
                for bb in range(GB):
                    w = wdn[:, c * D:(c + 1) * D] if c < NF - 1 else wdl[:]
                    last = nc.tensor.matmul(bank(Y_BANK[g % 2])[:, bb * D:(bb + 1) * D], ht[c][0:m, bb * T:(bb + 1) * T], w,
                                            start=c == 0 and bb == 0, stop=c == NF - 1, skip_group_check=True)
                if c == NF - 1:
                    last.then_inc(mm_y, 1)

            def step(s, h, g, phase, a, bc, d):
                par, b_par = phase % 2, 1 - phase % 2
                static = isinstance(s, int)

                late = not static or s > 2
                ffn = static and s == LAST - 1

                def read(r, before):
                    group, blk = before
                    if r < 2:
                        pe.wait_ge(qk_by_dve, dve_count(group, blk, r))
                    else:
                        pe.wait_ge(qk_by_act, act_count(group, blk, r))

                def read_k2(r, blk):
                    if r < 2:
                        pe.wait_ge(k2_by_dve, k2_dve_count(g, blk, r))
                    else:
                        pe.wait_ge(k2_by_act, k2_act_count(g, blk, r))

                def ring_wait(r):
                    if phase == 0 and a:
                        read(r, (g, "D"))
                    elif phase == 1 and a:
                        read_k2(r, "F")
                    elif r == 1 and late:
                        pe.wait_ge(sum2x_ready, s - 2)
                    elif r == 2:
                        pe.wait_ge(s2_ready, s - 1)

                def transpose_p(u):
                    if u % 2 == 0:
                        pe.wait_ge(p_ready, 2 * s - 2 + u // 2 + 1)
                    for i in range(4):
                        hd = 4 * u + i
                        last = nc.tensor.transpose(bank(T_BANK[u])[:, i * T:(i + 1) * T], p[:, hd * T:(hd + 1) * T], ident[:])
                    last.then_inc(mm_t, 1)

                if static and s == 0:
                    pe.wait_ge(x_lo, 1)
                    pe.wait_ge(w_lo, WQK_SPLIT[0])
                    project_qk(0, "A", lambda r: None, FIRST_BANKS)
                    pe.wait_ge(w_lo, WQK_SPLIT[1])
                    project_qk(0, "B", lambda r: None)
                    pe.wait_ge(w_lo, WQK_SPLIT[2])
                if static and s == 1:
                    pe.wait_ge(in_ident, 16)
                if bc:
                    transpose_p(0)
                    transpose_p(1)
                if phase == 0 and a and bc:
                    project_qk(g, "B", lambda r: pe.wait_ge(s2_ready, s - 1), units=(2, 3))
                if phase == 1 and a:
                    project_k2(g, "E", lambda r: None if static else pe.wait_ge(s2_ready, s - 1), units=(2, 3))
                if phase == 0 and a:
                    project_qk(g, "C", lambda r: read(r, (g, "B")))
                    if static and s == 0:
                        pe.wait_ge(w_lo, WQK_SPLIT[3])
                if bc:
                    transpose_p(2)
                    transpose_p(3)
                if phase == 0 and a:
                    project_qk(g, "D", lambda r: read(r, (g, "C")))
                if phase == 1 and a:
                    project_k2(g, "F", lambda r: read_k2(r, "E"))
                if a:
                    if static and s == 0:
                        pe.wait_ge(w_lo, WV_SPLIT)
                    if bc:
                        pe.wait_ge(pt_ready, 4 * s - 4 + 2)
                    own = slice(phase * T, (phase + 1) * T)
                    for u in range(2):
                        cols = slice(u * BANK, (u + 1) * BANK)
                        nc.tensor.matmul(bank(V_BANK[u]), xg_lo[:, own], wv_hi[:, cols], start=True, stop=False)
                        nc.tensor.matmul(bank(V_BANK[u]), xg_hi[:, own], wv_hi[:, cols], start=False, stop=False)
                        nc.tensor.matmul(bank(V_BANK[u]), xg_hi[:, own], wv_lo[:, cols], start=False, stop=True).then_inc(mm_v, 1)
                if bc:
                    for u in range(2):
                        pe.wait_ge(pt_ready, 4 * s - 4 + u + 3)
                        if u == 0:
                            pe.wait_ge(v_ready, 2 * s)
                        for i in range(8):
                            hd = 8 * u + i
                            last = nc.tensor.matmul(bank(PV_BANK[u])[64 * (i % 2):64 * (i % 2) + 64, (i // 2) * T:(i // 2 + 1) * T],
                                                    v[b_par][:, hd * DH:(hd + 1) * DH], pt[:, hd * T:(hd + 1) * T], start=True, stop=True)
                        last.then_inc(mm_pv, 1)
                if bc:
                    if static and s == 1:
                        pe.wait_ge(w_lo, WV2_SPLIT)
                    own = slice((phase - 1) % GB * T, ((phase - 1) % GB + 1) * T)
                    for u in range(2):
                        ring_wait(u)
                        cols = slice(u * BANK, (u + 1) * BANK)
                        nc.tensor.matmul(bank(V2[u]), cg_lo[:, own], wv2_hi[:, cols], start=True, stop=False)
                        nc.tensor.matmul(bank(V2[u]), cg_hi[:, own], wv2_hi[:, cols], start=False, stop=False)
                        nc.tensor.matmul(bank(V2[u]), cg_hi[:, own], wv2_lo[:, cols], start=False, stop=True).then_inc(mm_v2, 1)
                    if static and s == 1:
                        pe.wait_ge(in_wo, 16)
                    if late:
                        if a:
                            pe.wait_ge(v_ready, 2 * s + 1)
                        transpose_x2(s - 1, V_BANK[0])
                    ring_wait(2)
                    pe.wait_ge(ot_ready, 2 * s)
                    for c in range(NC):
                        last = nc.tensor.matmul(bank(O, D), ot[:, c * T:(c + 1) * T], wo[:, c * D:(c + 1) * D],
                                                start=c == 0, stop=c == NC - 1)
                    last.then_inc(mm_o, 1)
                if d:
                    ring_wait(3)
                    transpose_p2(s)
                if ffn:
                    pe.wait_ge(wup_split, 2)
                    pe.wait_ge(f_lo, 1)
                    up(0, 0)
                    up(0, 1)
                if a and phase == 0:
                    read(1, (g, "D"))
                    read(3, (g, "D"))
                if a:
                    pe.wait_ge(v_ready, 2 * s + 2)
                    if late:
                        pe.wait_ge(xnt_ready, s - 2)
                    for half in range(2):
                        for i in range(8):
                            hd = 8 * half + i
                            rows = slice(64 * (i % 2), 64 * (i % 2) + 64)
                            cols = slice(((hd // 2) * GB + phase) * T, ((hd // 2) * GB + phase + 1) * T)
                            mm = nc.tensor.matmul(bank(S_BANK[2 * half + i % 2])[:, (i // 2) * T:(i // 2 + 1) * T],
                                                  qt[rows, cols], kt[rows, cols], start=True, stop=True)
                            if i >= 6:
                                mm.then_inc(mm_s, 1)
                if bc:
                    if static and s == 1:
                        pe.wait_ge(in_perm, 16)
                    pe.wait_ge(v2s_ready, 2 * s - 2 + 1)
                    pe.wait_ge(x1_ready, s)
                    nc.tensor.transpose(bank(X1T, T), x1[:], perm[:]).then_inc(mm_x1t, 1)

                def project_q2(u):
                    for c in range(4):
                        last = nc.tensor.matmul(bank(Q2[u])[:, c * T:(c + 1) * T],
                                                wq2[:, (4 * u + c) * 128:(4 * u + c + 1) * 128], x1t[:], start=True, stop=True)
                    last.then_inc(mm_q2, 1)

                if d:
                    pe.wait_ge(v2_moved, 16 * 16 * (s - 1))
                    pe.wait_ge(v2s_ready, 2 * s)
                    weighted_v2(s, 0)
                if ffn:
                    pe.wait_ge(xnt_ready, s - 2)
                    down(0, 0)
                    up(0, 2)
                if bc:
                    if static and s == 1:
                        pe.wait_ge(in_wq2, 16)
                    if d:
                        pe.wait_ge(pb_ready, 2 * (s - 2) + 2)
                    pe.wait_ge(x1t_ready, s)
                    project_q2(0)
                if d:
                    pe.wait_ge(sum1_ready, s)
                    weighted_v2(s, 1)
                if ffn:
                    down(0, 1)
                    up(0, 3)
                if bc:
                    project_q2(1)
                if ffn:
                    down(0, 2)
                    up(0, 4)
                if phase == 3 and not static:
                    pe.wait_ge(x_lo, g + 2)
                    after = [(ot2_by_act, s - 1), (q2_ready, 2 * s - 1), (ot2_by_dve, s - 1), (q2_ready, 2 * s)]
                    project_qk(g + 1, "A", lambda r: pe.wait_ge(*after[r]))
                    read(0, (g + 1, "A"))
                if d:
                    if static and s == 2:
                        pe.wait_ge(in_wo2, 16)
                    project_o2(s)
                if ffn:
                    down(0, 3)
                if phase == 3 and not static:
                    read(1, (g + 1, "A"))
                    read(2, (g + 1, "A"))
                if bc:
                    pe.wait_ge(sum1_ready, s)
                    pe.wait_ge(q2_ready, 2 * s)
                    if phase == 1:
                        read_k2(1, "F")
                        read_k2(3, "F")
                    for i in range(K * 2):
                        k, pp = i // 2, i % 2
                        first = ((phase - 1) % GB * K * 2 + i) * 2 * J * H
                        last = nc.tensor.matmul(bank(S2, BANK, 2)[64 * pp:64 * pp + 64, k * 128:(k + 1) * 128],
                                                qt2[:, i * J * H:(i + 1) * J * H], kb[:, first:first + 128], start=True, stop=True)
                    last.then_inc(mm_s2, 1)
                if ffn:
                    down(0, 4)
                if phase == 3 and not static:
                    project_qk(g + 1, "B", lambda r: read(3, (g + 1, "A")) if r == 0 else pe.wait_ge(sum2x_ready, s - 1),
                               units=(0, 1))
                if phase == 0 and a:
                    if static and s == 0:
                        pe.wait_ge(w_lo, WK2_SPLIT)
                    pe.wait_ge(c_lo, g + 1)

                    def before_e(r):
                        if static and s == 0:
                            read(r, (0, "D"))
                        elif r == 1:
                            pe.wait_ge(sum2x_ready, s - 1)

                    project_k2(g, "E", before_e, units=(0, 1))

            run_steps(pe, step)
            for g in range(1, NG):
                pe.wait_ge(f_lo, g + 1 if g < NG - 1 else g + 2)
                up(g, 0)
                up(g, 1)
                for c in range(NF):
                    if (g, c) == (1, 3):
                        transpose_p2(LAST)
                        transpose_x2(LAST - 1, X2T_BANK)
                    if (g, c) == (2, 0):
                        pe.wait_ge(v2_moved, 16 * 16 * B)
                        weighted_v2(LAST, 0)
                        weighted_v2(LAST, 1)
                    if (g, c) == (2, 1):
                        project_o2(LAST)
                    down(g, c)
                    if c + 2 < NF:
                        up(g, c + 2)
                if g == 2:
                    pe.wait_ge(xnt_ready, B - 1)
                    transpose_x2(LAST, X2T_BANK)


def kernel(x, ctx_1024, L0_attn_W_Q, L0_attn_b_Q, L0_attn_W_K, L0_attn_b_K, L0_attn_W_V, L0_attn_b_V, L0_attn_W_O,
           L0_attn_b_O, L0_xattn_Wq, L0_xattn_bq, L0_xattn_Wk, L0_xattn_bk, L0_xattn_Wv, L0_xattn_bv, L0_xattn_Wo,
           L0_xattn_bo, L0_ffn_routing_token, L0_ffn_light_gamma, L0_ffn_light_w1, L0_ffn_light_b1, L0_ffn_light_w2,
           L0_ffn_light_b2, L0_ffn_heavy_gamma, L0_ffn_heavy_w1, L0_ffn_heavy_b1, L0_ffn_heavy_w2, L0_ffn_heavy_b2):
    import numpy as np
    import concourse.bacc as bacc
    from concourse.bass_utils import run_bass_kernel_spmd

    def a(z):
        return np.ascontiguousarray(np.asarray(z))

    def chunks(z):
        return a(np.asarray(z).reshape(-1, 128).T)

    order = np.arange(T).reshape(IH, J, 2, K).transpose(0, 3, 2, 1).reshape(-1)
    perm = np.zeros((T, T), np.float32)
    perm[order, np.arange(T)] = 1.0
    mask = np.zeros((128, K), np.float32)
    mask[np.arange(128), np.arange(128) // H] = 1.0
    own_j = np.zeros((128, J), np.float32)
    own_j[np.arange(128), np.arange(128) // H % J] = 1.0
    x = np.asarray(x)
    c = np.asarray(ctx_1024)
    b_up = np.zeros((128, NF), np.float32)
    b_up[:, 0:NF - 1] = np.asarray(L0_ffn_heavy_b1).reshape(NF - 1, 128).T
    b_up[0:FL, NF - 1] = np.asarray(L0_ffn_light_b1)
    arrays = {
        "x_nat": a(x),
        "x_t": a(x.reshape(NG, GB, T, D).transpose(0, 3, 1, 2).reshape(NG, D, GB * T)),
        "ctx_t": a(c[:, order, :].reshape(NG, GB, T, D).transpose(0, 3, 1, 2).reshape(NG, D, GB * T)),
        "w_qk": a(np.concatenate([np.asarray(L0_attn_W_Q).reshape(HD, D).T, np.asarray(L0_attn_W_K).reshape(HD, D).T], 1)),
        "w_v": a(np.asarray(L0_attn_W_V).reshape(HD, D).T),
        "w_o": a(np.asarray(L0_attn_W_O).transpose(0, 2, 1).reshape(NC, 128, D).transpose(1, 0, 2).reshape(128, NC * D)),
        "b_qk": a(np.concatenate([chunks(np.asarray(L0_attn_b_Q).reshape(-1)), chunks(np.asarray(L0_attn_b_K).reshape(-1))], 1)),
        "b_v": chunks(np.asarray(L0_attn_b_V).reshape(-1)),
        "b_o": a(L0_attn_b_O),
        "w2_q": a(np.asarray(L0_xattn_Wq).T),
        "w2_k": a(np.asarray(L0_xattn_Wk).T),
        "w2_v": a(np.asarray(L0_xattn_Wv).T),
        "w2_o": a(np.asarray(L0_xattn_Wo).reshape(D, 2, K, DH).transpose(1, 3, 2, 0).reshape(128, K * D)),
        "b2_q": chunks(L0_xattn_bq),
        "b2_k": chunks(L0_xattn_bk),
        "b2_v": a(L0_xattn_bv),
        "b2_o": a(L0_xattn_bo),
        "w_up": a(np.concatenate([np.asarray(L0_ffn_heavy_w1), np.asarray(L0_ffn_light_w1)], 1)),
        "g_light": a(np.asarray(L0_ffn_light_gamma).reshape(D, 1)),
        "g_heavy": a(np.asarray(L0_ffn_heavy_gamma).reshape(D, 1)),
        "w_down": a(np.asarray(L0_ffn_heavy_w2).reshape(NF - 1, 128, D).transpose(1, 0, 2).reshape(128, (NF - 1) * D)),
        "w_down_light": a(L0_ffn_light_w2),
        "b_up": b_up,
        "bd_light": a(L0_ffn_light_b2),
        "bd_heavy": a(L0_ffn_heavy_b2),
        "ident_in": np.eye(128, dtype=np.float32),
        "perm_in": perm,
        "mask_in": mask,
        "own_j_in": own_j,
    }
    nc = bacc.Bacc("TRN2", target_bir_lowering=False, num_devices=1)
    args = {n: nc.dram_tensor(n, z.shape, mybir.dt.from_np(z.dtype), kind="ExternalInput").ap() for n, z in arrays.items()}
    out = nc.dram_tensor("out", (B, T, D), mybir.dt.float32, kind="ExternalOutput").ap()
    build(nc, out=out, **args)
    r = run_bass_kernel_spmd(nc, [arrays], core_ids=[0])
    return r.results[0]["out"]
```
